# Optimizing a Trainium2 kernel written in Bass

```python
import numpy as np
import jax
import jax.numpy as jnp

def _softmax(x, axis=-1):
    return jax.nn.softmax(x, axis=axis)

def _gelu(x):
    return jax.nn.gelu(x, approximate=True)

def _silu(x):
    return jax.nn.silu(x)

def _sigmoid(x):
    return jax.nn.sigmoid(x)

def _layernorm(x, axis=-1, eps=1e-05):
    m = jnp.mean(x, axis=axis, keepdims=True)
    v = jnp.var(x, axis=axis, keepdims=True)
    return (x - m) / jnp.sqrt(v + eps)

def _scatter_add(tgt, idx, src, axis=0):
    return tgt.at[idx].add(src)

def _segment_sum(src, seg, n):
    return jax.ops.segment_sum(src, seg, n)
kernel_name = 'mk_adj_resnorm_d4_adj_r2_1140b7'

def setup_inputs(seed: int=0):
    np.random.seed(seed)
    _w = jnp.asarray

    def _rec_inputs():
        import jax
        import jax.numpy as jnp
        _gk = jax.random.key(seed)
        x = -0.0005207 + 1.001 * jax.random.normal(jax.random.fold_in(_gk, 1), (64, 128, 128), jnp.float32)
        _a = jax.random.bernoulli(jax.random.fold_in(_gk, 2), 0.015625, (128, 128))
        _a = jnp.logical_or(_a, jnp.swapaxes(_a, -1, -2))
        _a = jnp.logical_or(_a, jnp.eye(128, dtype=bool))
        _af = _a.astype(jnp.float32)
        adj = _af
        return (x, adj)
    x, adj = _rec_inputs()

    def _L0_gnn_setup():
        import jax, jax.numpy as jnp
        import numpy as np
        B, N, IN_DIM, OUT_DIM, H = (2, 2048, 128, 128, 4)
        HEAD_DIM = OUT_DIM // H
        EDGE_P = 0.01
        key = jax.random.key(seed)
        k1, k2, k3 = jax.random.split(key, 3)
        h = jax.random.normal(k1, (B, N, IN_DIM), dtype=jnp.float32)
        W = jax.random.normal(k2, (IN_DIM, 3 * OUT_DIM), dtype=jnp.float32) / np.sqrt(IN_DIM)
        adj = (jax.random.uniform(k3, (N, N)) < EDGE_P).astype(jnp.float32)
        adj = jnp.maximum(adj, jnp.eye(N, dtype=jnp.float32))
        return {'h': h, 'W': W, 'adj': adj}
    _L0_gnn_all = _L0_gnn_setup()
    _L0_gnn_in = {k: v for k, v in _L0_gnn_all.items() if k in ('W',)}
    del _L0_gnn_all

    def _L1_gnn_setup():
        import jax, jax.numpy as jnp
        import numpy as np
        B, J, F_IN, F_OUT = (8192, 17, 128, 128)
        key = jax.random.key(seed)
        k1, k2, k3, k4 = jax.random.split(key, 4)
        gain = 1.414
        bound = gain * np.sqrt(6.0 / (F_IN + F_OUT))
        W = jax.random.uniform(k2, (3, F_IN, F_OUT), dtype=jnp.float32, minval=-bound, maxval=bound)
        stdv = 1.0 / np.sqrt(F_OUT)
        bias = jax.random.uniform(k4, (F_OUT,), dtype=jnp.float32, minval=-stdv, maxval=stdv)
        return {'x': jax.random.normal(k1, (B, J, F_IN), dtype=jnp.float32), 'W': W, 'adj': jax.random.uniform(k3, (J, J), dtype=jnp.float32), 'bias': bias}
    _L1_gnn_all = _L1_gnn_setup()
    _L1_gnn_in = {k: v for k, v in _L1_gnn_all.items() if k in ('W', 'bias')}
    del _L1_gnn_all

    def _L2_gnn_setup():
        import jax, jax.numpy as jnp
        import numpy as np
        EPS = 1e-05

        def _batchnorm(x, gamma, beta):
            mu = jnp.mean(x, axis=0)
            var = jnp.var(x, axis=0)
            return (x - mu) * jax.lax.rsqrt(var + EPS) * gamma + beta
        key = jax.random.key(seed)
        ks = jax.random.split(key, 4)
        b, n, d, h, o = (32, 1024, 128, 256, 128)
        features = jax.random.normal(ks[0], (b, n, d), dtype=jnp.float32)
        A = jax.random.uniform(ks[1], (n, n), dtype=jnp.float32)
        lim1 = float(np.sqrt(6.0 / (d + h)))
        W1 = jax.random.uniform(ks[2], (h, d), minval=-lim1, maxval=lim1, dtype=jnp.float32)
        b1 = jnp.zeros((h,), jnp.float32)
        lim2 = float(np.sqrt(6.0 / (h + o)))
        W2 = jax.random.uniform(ks[3], (o, h), minval=-lim2, maxval=lim2, dtype=jnp.float32)
        b2 = jnp.zeros((o,), jnp.float32)
        g1 = jnp.ones((h,), jnp.float32)
        be1 = jnp.zeros((h,), jnp.float32)
        g2 = jnp.ones((o,), jnp.float32)
        be2 = jnp.zeros((o,), jnp.float32)
        return {'features': features, 'A': A, 'W1': W1, 'b1': b1, 'g1': g1, 'be1': be1, 'W2': W2, 'b2': b2, 'g2': g2, 'be2': be2}
    _L2_gnn_all = _L2_gnn_setup()
    _L2_gnn_in = {k: v for k, v in _L2_gnn_all.items() if k in ('W1', 'b1', 'g1', 'be1', 'W2', 'b2', 'g2', 'be2')}
    del _L2_gnn_all

    def _L3_gnn_setup():
        import jax, jax.numpy as jnp
        import numpy as np
        B, T, D, H = (64, 1024, 128, 128)
        MAX_SKIP = 4

        def _lstm_last(Wih, Whh, bih, bhh, xs):
            N, _, Hd = xs.shape
            bias = bih + bhh

            def step(carry, x_t):
                h, c = carry
                g = x_t @ Wih.T + h @ Whh.T + bias
                i, f, gg, o = jnp.split(g, 4, axis=-1)
                c = jax.nn.sigmoid(f) * c + jax.nn.sigmoid(i) * jnp.tanh(gg)
                h = jax.nn.sigmoid(o) * jnp.tanh(c)
                return ((h, c), None)
            init = (jnp.zeros((N, Hd), xs.dtype), jnp.zeros((N, Hd), xs.dtype))
            (h_last, _), _ = jax.lax.scan(step, init, jnp.swapaxes(xs, 0, 1))
            return h_last
        key = jax.random.key(seed)
        ks = jax.random.split(key, 8)
        s = 0.05
        x = jax.random.normal(ks[0], (B, T, D), jnp.float32)
        adj = jax.random.uniform(ks[1], (T, T), jnp.float32) / T
        Wg0 = jax.random.normal(ks[2], (D, H), jnp.float32) * s
        bg0 = jnp.zeros((H,), jnp.float32)
        Wg1 = jax.random.normal(ks[3], (H, H), jnp.float32) * s
        bg1 = jnp.zeros((H,), jnp.float32)
        Wih = jax.random.normal(ks[4], (MAX_SKIP, 4 * H, H), jnp.float32) * s
        Whh = jax.random.normal(ks[5], (MAX_SKIP, 4 * H, H), jnp.float32) * s
        bih = jax.random.normal(ks[6], (MAX_SKIP, 4 * H), jnp.float32) * s
        bhh = jax.random.normal(ks[7], (MAX_SKIP, 4 * H), jnp.float32) * s
        return dict(x=x, adj=adj, Wg0=Wg0, bg0=bg0, Wg1=Wg1, bg1=bg1, Wih=Wih, Whh=Whh, bih=bih, bhh=bhh)
    _L3_gnn_all = _L3_gnn_setup()
    _L3_gnn_in = {k: v for k, v in _L3_gnn_all.items() if k in ('Wg0', 'bg0', 'Wg1', 'bg1', 'Wih', 'Whh', 'bih', 'bhh')}
    del _L3_gnn_all
    return {'x': x, 'adj': adj, 'L0_gnn_W': _L0_gnn_in['W'], 'L1_gnn_W': _L1_gnn_in['W'], 'L1_gnn_bias': _L1_gnn_in['bias'], 'L2_gnn_W1': _L2_gnn_in['W1'], 'L2_gnn_b1': _L2_gnn_in['b1'], 'L2_gnn_g1': _L2_gnn_in['g1'], 'L2_gnn_be1': _L2_gnn_in['be1'], 'L2_gnn_W2': _L2_gnn_in['W2'], 'L2_gnn_b2': _L2_gnn_in['b2'], 'L2_gnn_g2': _L2_gnn_in['g2'], 'L2_gnn_be2': _L2_gnn_in['be2'], 'L3_gnn_Wg0': _L3_gnn_in['Wg0'], 'L3_gnn_bg0': _L3_gnn_in['bg0'], 'L3_gnn_Wg1': _L3_gnn_in['Wg1'], 'L3_gnn_bg1': _L3_gnn_in['bg1'], 'L3_gnn_Wih': _L3_gnn_in['Wih'], 'L3_gnn_Whh': _L3_gnn_in['Whh'], 'L3_gnn_bih': _L3_gnn_in['bih'], 'L3_gnn_bhh': _L3_gnn_in['bhh']}

def reference(x, adj, L0_gnn_W, L1_gnn_W, L1_gnn_bias, L2_gnn_W1, L2_gnn_b1, L2_gnn_g1, L2_gnn_be1, L2_gnn_W2, L2_gnn_b2, L2_gnn_g2, L2_gnn_be2, L3_gnn_Wg0, L3_gnn_bg0, L3_gnn_Wg1, L3_gnn_bg1, L3_gnn_Wih, L3_gnn_Whh, L3_gnn_bih, L3_gnn_bhh):
    import jax
    import jax.numpy as jnp

    def _L0_gnn_ref(h, W, adj):
        import jax, jax.numpy as jnp
        import numpy as np
        B, N, IN_DIM, OUT_DIM, H = (2, 2048, 128, 128, 4)
        HEAD_DIM = OUT_DIM // H
        EDGE_P = 0.01
        Bn, Nn, _ = h.shape
        qkv = h @ W
        qkv = qkv.reshape(Bn, Nn, 3, H, HEAD_DIM).transpose(2, 0, 3, 1, 4)
        q, k, v = (qkv[0], qkv[1], qkv[2])
        mask = jnp.where(adj == 0, -jnp.inf, 0.0)
        scores = jnp.einsum('bhid,bhjd->bhij', q, k) / np.sqrt(HEAD_DIM) + mask
        attn = jax.nn.softmax(scores, axis=-1)
        out = jnp.einsum('bhij,bhjd->bhid', attn, v)
        return out.transpose(0, 2, 1, 3).reshape(Bn, Nn, OUT_DIM)

    def _L1_gnn_ref(x, W, adj, bias):
        import jax, jax.numpy as jnp
        import numpy as np
        B, J, F_IN, F_OUT = (8192, 17, 128, 128)
        adj_0 = jnp.diag(jnp.diagonal(adj))
        adj_1 = jnp.triu(adj, k=1)
        adj_2 = jnp.tril(adj, k=-1)
        h = jnp.einsum('bjf,kfo->kbjo', x, W)
        out = jnp.einsum('ij,bjo->bio', adj_0, h[0]) + jnp.einsum('ij,bjo->bio', adj_1, h[1]) + jnp.einsum('ij,bjo->bio', adj_2, h[2])
        return out + bias[None, None, :]

    def _L2_gnn_ref(features, A, W1, b1, g1, be1, W2, b2, g2, be2):
        import jax, jax.numpy as jnp
        import numpy as np
        EPS = 1e-05

        def _batchnorm(x, gamma, beta):
            mu = jnp.mean(x, axis=0)
            var = jnp.var(x, axis=0)
            return (x - mu) * jax.lax.rsqrt(var + EPS) * gamma + beta
        b, n, d = features.shape
        A_norm = A + jnp.eye(n, dtype=A.dtype)
        deg = jnp.sum(A_norm, axis=0) + jnp.sum(A_norm, axis=1) - jnp.diagonal(A_norm)
        dinv = jax.lax.rsqrt(deg)
        A_hat = A_norm * dinv[:, None] * dinv[None, :]
        agg = jnp.einsum('nm,bmd->bnd', A_hat, features)
        x = agg.reshape(-1, d)
        h = jax.nn.relu(_batchnorm(x @ W1.T + b1, g1, be1))
        out = h @ W2.T + b2
        out = _batchnorm(out, g2, be2)
        return out.reshape(b, n, -1)

    def _L3_gnn_ref(x, adj, Wg0, bg0, Wg1, bg1, Wih, Whh, bih, bhh):
        import jax, jax.numpy as jnp
        import numpy as np
        B, T, D, H = (64, 1024, 128, 128)
        MAX_SKIP = 4

        def _lstm_last(Wih, Whh, bih, bhh, xs):
            N, _, Hd = xs.shape
            bias = bih + bhh

            def step(carry, x_t):
                h, c = carry
                g = x_t @ Wih.T + h @ Whh.T + bias
                i, f, gg, o = jnp.split(g, 4, axis=-1)
                c = jax.nn.sigmoid(f) * c + jax.nn.sigmoid(i) * jnp.tanh(gg)
                h = jax.nn.sigmoid(o) * jnp.tanh(c)
                return ((h, c), None)
            init = (jnp.zeros((N, Hd), xs.dtype), jnp.zeros((N, Hd), xs.dtype))
            (h_last, _), _ = jax.lax.scan(step, init, jnp.swapaxes(xs, 0, 1))
            return h_last
        h = jax.nn.relu(jnp.einsum('ts,bsh->bth', adj, x @ Wg0 + bg0))
        h = jax.nn.relu(jnp.einsum('ts,bsh->bth', adj, h @ Wg1 + bg1))
        Bv, Tv, Hd = h.shape
        for p in range(1, MAX_SKIP + 1):
            nw = Tv // p
            wins = h[:, :nw * p, :].reshape(Bv * nw, p, Hd)
            last = _lstm_last(Wih[p - 1], Whh[p - 1], bih[p - 1], bhh[p - 1], wins)
            idx = jnp.arange(nw) * p + (p - 1)
            h = h.at[:, idx, :].set(last.reshape(Bv, nw, Hd))
        return h
    x = _layernorm(x + _L0_gnn_ref(x, L0_gnn_W, adj), axis=-1)
    x = _layernorm(x + _L1_gnn_ref(x, L1_gnn_W, adj, L1_gnn_bias), axis=-1)
    x = _layernorm(x + _L2_gnn_ref(x, adj, L2_gnn_W1, L2_gnn_b1, L2_gnn_g1, L2_gnn_be1, L2_gnn_W2, L2_gnn_b2, L2_gnn_g2, L2_gnn_be2), axis=-1)
    x = _layernorm(x + _L3_gnn_ref(x, adj, L3_gnn_Wg0, L3_gnn_bg0, L3_gnn_Wg1, L3_gnn_bg1, L3_gnn_Wih, L3_gnn_Whh, L3_gnn_bih, L3_gnn_bhh), axis=-1)
    return x

_drawn_inputs = setup_inputs


def setup_inputs(seed=0):
    import zlib

    import numpy as np

    out = dict(_drawn_inputs(seed))
    spreads = {'L2_gnn_b1': (0.0, 0.8),
     'L2_gnn_g1': (1.0, 0.2),
     'L2_gnn_be1': (0.0, 0.1),
     'L2_gnn_b2': (0.0, 0.8),
     'L2_gnn_g2': (1.0, 0.2),
     'L2_gnn_be2': (0.0, 0.1),
     'L3_gnn_bg0': (0.0, 0.1),
     'L3_gnn_bg1': (0.0, 0.332)}
    factors = {'L1_gnn_bias': 4.667, 'L3_gnn_Whh': 8.0, 'L3_gnn_bih': 2.958, 'L3_gnn_bhh': 2.99}
    for name, (base, spread) in spreads.items():
        noise = np.random.default_rng([zlib.crc32(name.encode()), seed]).standard_normal(out[name].shape)
        drawn = base * np.exp(spread * noise) if base else spread * noise
        out[name] = jnp.asarray(drawn.astype(out[name].dtype))
    for name, factor in factors.items():
        out[name] = (out[name] * factor).astype(out[name].dtype)
    return out
```

```python
from contextlib import ExitStack

import concourse.bass as bass
from concourse import mybir

F32 = mybir.dt.float32
ALU = mybir.AluOpType
ACT = mybir.ActivationFunctionType
AX_X = mybir.AxisListType.X

B, N, D = 64, 128, 128
HEADS = 4
HD = D // HEADS
VW = HD + 2
GB = 4
G = B // GB
T = GB * N
TOKENS = B * N
HID = 2
STEPS = 4
GATES = 4
EPS = 1e-5
MASKED = -1.0e30



def ds(start, size):
    return bass.ds(start, size)


def need(eng, sem, value):
    if isinstance(value, int) and value <= 0:
        return
    eng.wait_ge(sem, value)


class Turn:

    def __init__(self, m, c, peeled):
        self.m, self.c, self.peeled = m, c, peeled

    def group(self, lag):
        return self.m * 2 + (self.c - lag)

    def half(self, lag):
        return self.m + (self.c - lag) // 2

    def par(self, lag):
        return (self.c - lag) % 2

    def has(self, lag):
        return not self.peeled or 0 <= self.c - lag < G


def turns(eng, body, first, steady, steady_end, last):
    for c in range(first, steady):
        body(Turn(0, c, True))
    with eng.Fori(0, (steady_end - steady) // 2) as m:
        for u in range(2):
            body(Turn(m, steady + u, False))
    for c in range(steady_end, last):
        body(Turn(0, c, True))


def build(nc, io):
    with ExitStack() as ctx:
        def sb(name, shape):
            return ctx.enter_context(nc.sbuf_tensor(name, shape, F32))

        def sem(name):
            return ctx.enter_context(nc.semaphore(name))

        bank = [ctx.enter_context(nc.psum_tensor(f"bank{i}", [128, 512], F32)) for i in range(8)]

        wqkv = sb("wqkv", [D, 3 * D])
        w_l1 = sb("w_l1", [D, 3, D])
        w1t = sb("w1t", [D, HID * 128])
        w2t = sb("w2t", [128, HID, D])
        wg = sb("wg", [D, 2, D])
        wiht = sb("wiht", [D, STEPS, GATES * D])
        whht = sb("whht", [D, STEPS, GATES * D])
        adj = sb("adj", [N, N])
        adjt = sb("adjt", [N, N])
        bn1p = sb("bn1p", [128, 3, HID])
        bn2p = sb("bn2p", [128, 3])
        lstm_b = sb("lstm_b", [D, 2, STEPS * GATES])
        gate_bias = sb("gate_bias", [D, STEPS * GATES])
        rows = sb("rows", [1, 3, D])
        row_bias = sb("row_bias", [128, 3, D])
        ident = sb("ident", [128, 128])
        ones_row = sb("ones_row", [1, 128])
        eps_wide = sb("eps_wide", [128, 2 * GB])
        neg_half_wide = sb("neg_half_wide", [128, 2 * GB])
        eps_tile, neg_half = eps_wide[:, 0:GB], neg_half_wide[:, 0:GB]
        bn_tmp = sb("bn_tmp", [128, HID + 1])
        idle_words = sb("idle_words", [128, 8])
        mask = sb("mask", [N, N])
        adj_split_t = sb("adj_split_t", [N, 3, N])
        ahat_t = sb("ahat_t", [N, N])
        anorm = sb("anorm", [N, N])
        anorm_t = sb("anorm_t", [N, N])
        degs = sb("degs", [N, 8])
        bn_stats1 = sb("bn_stats1", [128, HID, G, 6])
        bn_stats2 = sb("bn_stats2", [128, G, 6])
        bn_fin = sb("bn_fin", [128, 3, 6])

        xres = sb("xres", [N, B, D])
        wide = sb("wide", [128, 2, TOKENS])

        work = sb("work", [128, 18688])
        spot = [0]

        def carve(*shape):
            n = 1
            for s in shape:
                n *= s
            a = work[:, spot[0]:spot[0] + n]
            spot[0] += n
            assert spot[0] <= 18688, spot
            if len(shape) == 2:
                a = a.rearrange("p (a b) -> p a b", b=shape[1])
            elif len(shape) == 3:
                a = a.rearrange("p (a b c) -> p a b c", b=shape[1], c=shape[2])
            return a

        adj_loaded = sem("adj_loaded")
        weights_loaded = sem("weights_loaded")
        WEIGHT_LOADS = 11
        pool_setup = sem("pool_setup")
        dve_setup = sem("dve_setup")
        pe_setup = sem("pe_setup")

        with nc.Block() as block:
            @block.sync
            def _(sp):
                sp.dma_start(adj[:], io["adj"]).then_inc(adj_loaded, 16)
                sp.dma_start(adjt[:], io["adjt"]).then_inc(adj_loaded, 16)
                for tile, name in ((wqkv, "wqkv"), (w_l1, "w_l1"), (rows, "rows"), (w1t, "w1t"), (w2t, "w2t"),
                                   (wg, "wg"), (wiht, "wiht"), (whht, "whht"), (bn1p, "bn1p"), (bn2p, "bn2p"),
                                   (lstm_b, "lstm_b")):
                    sp.dma_start(tile[:], io[name]).then_inc(weights_loaded, 16)

            @block.gpsimd
            def _(pool):
                pool.memset(ident[:], 0.0).then_inc(pool_setup, 1)
                pool.memset(ones_row[:], 1.0).then_inc(pool_setup, 1)
                pool.memset(neg_half_wide[:], -0.5).then_inc(pool_setup, 1)
                pool.memset(eps_wide[:], EPS).then_inc(pool_setup, 1)
                pool.wait_ge(pool_setup, 4)
                pool.affine_select(out=ident[:], in_=ident[:], compare_op=ALU.not_equal, fill=1.0, base=0,
                                   pattern=[[-1, N]], channel_multiplier=1).then_inc(pool_setup, 1)
                pool.wait_ge(adj_loaded, 32)
                pool.affine_select(out=adj_split_t[:, 0, :], in_=adjt[:], compare_op=ALU.is_equal, fill=0.0,
                                   base=0, pattern=[[-1, N]], channel_multiplier=1).then_inc(pool_setup, 1)
                pool.affine_select(out=adj_split_t[:, 1, :], in_=adjt[:], compare_op=ALU.is_gt, fill=0.0,
                                   base=0, pattern=[[-1, N]], channel_multiplier=1).then_inc(pool_setup, 1)
                pool.affine_select(out=adj_split_t[:, 2, :], in_=adjt[:], compare_op=ALU.is_gt, fill=0.0,
                                   base=0, pattern=[[1, N]], channel_multiplier=-1).then_inc(pool_setup, 1)
                pool.wait_ge(dve_setup, 8)
                pool.tensor_tensor(degs[:, 5:6], degs[:, 4:5], neg_half[:, 0:1], ALU.pow).then_inc(pool_setup, 1)

            @block.vector
            def _(dve):
                dve.wait_ge(adj_loaded, 32)
                dve.tensor_scalar(mask[:], adj[:], 0.0, MASKED, ALU.is_equal, ALU.mult).then_inc(dve_setup, 1)
                dve.wait_ge(pool_setup, 8)
                dve.tensor_tensor(anorm[:], adj[:], ident[:], ALU.add).then_inc(dve_setup, 1)
                dve.tensor_tensor(anorm_t[:], adjt[:], ident[:], ALU.add).then_inc(dve_setup, 1)
                dve.tensor_reduce(degs[:, 2:3], adj_split_t[:, 0, :], AX_X, ALU.add).then_inc(dve_setup, 1)
                dve.wait_ge(dve_setup, 4)
                dve.tensor_reduce(degs[:, 0:1], anorm[:], AX_X, ALU.add).then_inc(dve_setup, 1)
                dve.tensor_reduce(degs[:, 1:2], anorm_t[:], AX_X, ALU.add).then_inc(dve_setup, 1)
                dve.wait_ge(dve_setup, 6)
                dve.tensor_tensor(degs[:, 3:4], degs[:, 0:1], degs[:, 1:2], ALU.add).then_inc(dve_setup, 1)
                dve.wait_ge(dve_setup, 7)
                dve.scalar_tensor_tensor(degs[:, 4:5], degs[:, 3:4], -1.0, degs[:, 2:3],
                                         ALU.add, ALU.subtract).then_inc(dve_setup, 1)
                dve.wait_ge(pool_setup, 9)
                dve.tensor_scalar(anorm[:], anorm[:], degs[:, 5:6], None, ALU.mult).then_inc(dve_setup, 1)
                dve.wait_ge(pe_setup, 1)
                dve.tensor_scalar(ahat_t[:], bank[0][:, 0:N], degs[:, 5:6], None, ALU.mult).then_inc(dve_setup, 1)
                dve.wait_ge(pe_setup, 2)
                dve.tensor_copy(row_bias[:], bank[1][:, 0:3 * D].rearrange("p (a d) -> p a d", a=3)) \
                   .then_inc(dve_setup, 1)
                dve.wait_ge(weights_loaded, 16 * WEIGHT_LOADS)
                dve.tensor_tensor(gate_bias[:], lstm_b[:, 0, :], lstm_b[:, 1, :], ALU.add).then_inc(dve_setup, 1)

            @block.tensor
            def _(pe):
                pe.wait_ge(dve_setup, 9)
                pe.wait_ge(pool_setup, 5)
                pe.transpose(bank[0][:, 0:N], anorm[:], ident[:]).then_inc(pe_setup, 1)
                pe.wait_ge(weights_loaded, 16 * WEIGHT_LOADS)
                pe.matmul(bank[1][:, 0:3 * D], ones_row[:], rows[:].rearrange("p a d -> p (a d)"),
                          start=True, stop=True).then_inc(pe_setup, 1)

        P, A, L, Y, H = -1, 0, 1, 2, 3

        xt_in = carve(2, T)
        xg = carve(2, T)
        q_all = carve(T)
        q_head = carve(2, HEADS, T)
        k_t = carve(2, T)
        v_one = carve(2, GB, HEADS * VW)
        scores = carve(2, HEADS * N)
        neg_max = carve(2, HEADS)
        probs = carve(2, HEADS * N)
        probs_t = carve(2, HEADS * N)
        recip = carve(HEADS)
        attn = carve(2, T)
        s0 = carve(T)
        x1 = carve(2, T)
        x1b = carve(2, T)
        agg3 = carve(2, 3 * N)
        s1 = carve(T)
        x2 = carve(T)
        agg_t = carve(T)
        ln_st = carve(2, GB, 6)
        ln_mv = carve(2, GB, 2)
        ln_rs = carve(2, GB)

        xt_ld = [sem(f"xt_ld{i}") for i in range(2)]
        xg_ld = [sem(f"xg_ld{i}") for i in range(2)]
        qh_ld = [sem(f"qh_ld{i}") for i in range(2)]
        bufs_set = sem("bufs_set")
        q_mm, k_mm, v_mm = sem("q_mm"), sem("k_mm"), sem("v_mm")
        q_out, k_out, v_out = sem("q_out"), sem("k_out"), sem("v_out")
        score_mm, score_max, exp_done = sem("score_mm"), sem("score_max"), sem("exp_done")
        pt_mm, pt_out = sem("pt_mm"), sem("pt_out")
        av_mm, av_recip, av_out = sem("av_mm"), sem("av_recip"), sem("av_out")
        s0_done, st0, mv0, ve0, rs0, x1_done, x1b_done = (
            sem("s0_done"), sem("st0"), sem("mv0"), sem("ve0"), sem("rs0"), sem("x1_done"), sem("x1b_done"))
        y_mm, y_out, z_mm = sem("y_mm"), sem("y_out"), sem("z_mm")
        s1_done, st1, mv1, ve1, rs1, x2_done, x2_kept = (
            sem("s1_done"), sem("st1"), sem("mv1"), sem("ve1"), sem("rs1"), sem("x2_done"), sem("x2_kept"))
        g_mm, g_out, h_mm, h_out, h_stat = sem("g_mm"), sem("g_out"), sem("h_mm"), sem("h_out"), sem("h_stat")

        R0, R1, S0, S1, PTB, OB, YB, ZB = bank

        with nc.Block() as block:
            @block.sync
            def _(sp):
                def load_xt(par, group):
                    sp.dma_start(xt_in[:, par, :], io["xt"][:, ds(group * T, T)]).then_inc(xt_ld[par], 16)

                def load_xg(par, group):
                    sp.dma_start(xg[:, par, :], io["x"][:, ds(group * T, T)]).then_inc(xg_ld[par], 16)

                for g in range(2):
                    load_xt(g, g)
                    load_xg(g, g)
                sp.wait_ge(bufs_set, 2)

                def turn(t):
                    if t.has(P):
                        sp.wait_ge(bufs_set, 2)
                        need(sp, q_out, t.group(P) + 1)
                        need(sp, score_mm, (t.group(P) - 1) * GB)
                        for h in range(HEADS):
                            sp.dma_start(q_head[HD * h:HD * (h + 1), t.par(P), h, :],
                                         q_all[HD * h:HD * (h + 1), :]).then_inc(qh_ld[t.par(P)], 16)
                        if not t.peeled or t.c - P + 2 < G:
                            need(sp, v_mm, t.group(P) + 1)
                            load_xt(t.par(P), t.group(P) + 2)
                    if t.has(L) and (not t.peeled or t.c - L + 2 < G):
                        need(sp, s0_done, t.group(L) + 1)
                        load_xg(t.par(L), t.group(L) + 2)

                turns(sp, turn, -1, 3, G - 3, G + 1)

            @block.tensor
            def _(pe):
                pe.wait_ge(weights_loaded, 16 * WEIGHT_LOADS)

                def turn(t):
                    for j in range(GB):
                        s = t.group(A) * GB + j
                        if t.has(A):
                            if j == 0:
                                need(pe, qh_ld[t.par(A)], (t.half(A) + 1) * 16 * HEADS)
                                need(pe, k_out, t.group(A) + 1)
                            need(pe, score_max, s - 1)
                            out = (S0, S1)[j % 2]
                            for h in range(HEADS):
                                mm = pe.matmul(out[:, h * N:(h + 1) * N], q_head[:, t.par(A), h, j * N:(j + 1) * N],
                                               k_t[:, t.par(A), j * N:(j + 1) * N], start=True, stop=True)
                            mm.then_inc(score_mm, 1)
                        if t.has(Y):
                            if j == 0:
                                need(pe, x1_done, t.group(Y) + 1)
                            need(pe, y_out, t.group(Y) * GB + j)
                            pe.matmul(YB[:, 0:3 * N], x1[:, t.par(Y), j * D:(j + 1) * D],
                                      adj_split_t[:].rearrange("p a n -> p (a n)"),
                                      start=True, stop=True).then_inc(y_mm, 1)
                        lag = A if j >= 1 else L
                        if t.has(lag):
                            need(pe, exp_done, s)
                            need(pe, pt_out, s - 1)
                            for h in range(HEADS):
                                mm = pe.transpose(PTB[:, h * N:(h + 1) * N],
                                                  probs[:, (j + 1) % 2, h * N:(h + 1) * N], ident[:])
                            mm.then_inc(pt_mm, 1)
                        if t.has(P):
                            par = t.par(P)
                            if j == 0:
                                need(pe, xt_ld[par], (t.half(P) + 1) * 16)
                                need(pe, v_out, t.group(P))
                                need(pe, h_out, (t.group(P) - 4) * HID)
                                pe.matmul(R0[:], wqkv[:, 0:D], xt_in[:, par, :], start=True, stop=True) \
                                  .then_inc(q_mm, 1)
                            if j == 1:
                                need(pe, k_out, t.group(P))
                                need(pe, h_out, (t.group(P) - 4) * HID)
                                pe.matmul(R1[:], wqkv[:, D:2 * D], xt_in[:, par, :], start=True, stop=True) \
                                  .then_inc(k_mm, 1)
                            if j == 2:
                                need(pe, q_out, t.group(P) + 1)
                                for b in range(GB):
                                    mm = pe.matmul(R0[:, b * D:(b + 1) * D], xt_in[:, par, b * N:(b + 1) * N],
                                                   wqkv[:, 2 * D:3 * D], start=True, stop=True)
                                mm.then_inc(v_mm, 1)
                        lag = A if j >= 2 else L
                        if t.has(lag):
                            vb = (j - 2) % GB
                            need(pe, pt_out, s - 1)
                            need(pe, av_out, s - 2)
                            need(pe, v_out, t.group(lag) + 1)
                            for h in range(HEADS):
                                mm = pe.matmul(OB[:, h * VW:(h + 1) * VW], probs_t[:, j % 2, h * N:(h + 1) * N],
                                               v_one[:, t.par(lag), vb, h * VW:(h + 1) * VW], start=True, stop=True)
                            mm.then_inc(av_mm, 1)
                        if t.has(H) and j == 2:
                            need(pe, x2_done, t.group(H) + 1)
                            need(pe, h_out, t.group(H) * HID)
                            if t.has(P):
                                need(pe, k_out, t.group(P) + 1)
                            for b in range(GB):
                                mm = pe.matmul(R1[:, b * N:(b + 1) * N], x2[:, b * D:(b + 1) * D],
                                               ahat_t[:], start=True, stop=True)
                            mm.then_inc(g_mm, 1)
                        if t.has(H) and j == 3:
                            need(pe, g_out, t.group(H) + 1)
                            need(pe, h_out, t.group(H) * HID)
                            if t.has(P):
                                need(pe, v_out, t.group(P) + 1)
                            for k, out in enumerate((R0, R1)):
                                pe.matmul(out[:], w1t[:, k * 128:(k + 1) * 128], agg_t[:], start=True, stop=True) \
                                  .then_inc(h_mm, 1)
                        if t.has(Y):
                            need(pe, y_out, t.group(Y) * GB + j + 1)
                            if j == 0:
                                need(pe, s1_done, t.group(Y))
                            for k in range(3):
                                mm = pe.matmul(ZB[:, j * D:(j + 1) * D], agg3[:, j % 2, k * N:(k + 1) * N],
                                               w_l1[:, k, :], start=(k == 0), stop=(k == 2))
                            mm.then_inc(z_mm, 1)

                turns(pe, turn, -1, 4, G - 2, G + 3)

            @block.scalar
            def _(act):
                def turn(t):
                    for j in range(GB):
                        s = t.group(A) * GB + j
                        if t.has(Y):
                            y = t.group(Y) * GB + j
                            need(act, y_mm, y + 1)
                            need(act, z_mm, y - 1)
                            act.copy(agg3[:, j % 2, :], YB[:, 0:3 * N]).then_inc(y_out, 1)
                        if t.has(P) and j == 0:
                            need(act, q_mm, t.group(P) + 1)
                            need(act, qh_ld[1 - t.par(P)], t.half(P + 1) * 16 * HEADS + 16 * HEADS)
                            act.mul(q_all, R0[:], HD ** -0.5).then_inc(q_out, 1)
                        if t.has(A):
                            need(act, score_max, s + 1)
                            need(act, pt_mm, s - 1)
                            for h in range(HEADS):
                                e = act.activation(probs[:, j % 2, h * N:(h + 1) * N],
                                                   scores[:, j % 2, h * N:(h + 1) * N], ACT.Exp,
                                                   bias=neg_max[:, j % 2, h:h + 1], scale=-1.0)
                            e.then_inc(exp_done, 1)
                        if t.has(H) and j == 2:
                            need(act, g_mm, t.group(H) + 1)
                            need(act, h_mm, t.group(H) * HID)
                            act.copy(agg_t, R1[:]).then_inc(g_out, 1)
                        if t.has(H) and j == 3:
                            for k, src in enumerate((R0, R1)):
                                need(act, h_mm, t.group(H) * HID + k + 1)
                                act.activation(wide[:, k, ds(t.group(H) * T, T)], src[:], ACT.Identity,
                                               bias=bn1p[:, 0, k:k + 1]).then_inc(h_out, 1)

                turns(act, turn, -1, 4, G - 2, G + 3)

            @block.vector
            def _(dve):
                def carry_waits(word):
                    dve.memset(idle_words[:, word:word + 1], 0.0)

                dve.memset(q_head.rearrange("p a h t -> p (a h t)"), 0.0).then_inc(bufs_set, 1)
                dve.memset(v_one.rearrange("p a b v -> p (a b v)"), 1.0).then_inc(bufs_set, 1)
                dve.wait_ge(bufs_set, 2)

                def ln_stats(i, src, stat_sem, mv_sem, group):
                    for b in range(GB):
                        dve.bn_stats(ln_st[:, i, b, :], src[:, b * D:(b + 1) * D]).then_inc(stat_sem, 1)
                    need(dve, stat_sem, (group + 1) * GB)
                    carry_waits(GB + i)
                    for b in range(GB):
                        dve.bn_aggr(ln_mv[:, i, b, :], ln_st[:, i, b, :]).then_inc(mv_sem, 1)

                def ln_apply(i, src, dst, done):
                    for b in range(GB):
                        op = dve.tensor_scalar(dst[:, b * D:(b + 1) * D], src[:, b * D:(b + 1) * D],
                                               ln_mv[:, i, b, 0:1], ln_rs[:, i, b:b + 1], ALU.subtract, ALU.mult)
                    op.then_inc(done, 1)

                def turn(t):
                    for j in range(GB):
                        s = t.group(A) * GB + j
                        if t.has(A):
                            need(dve, score_mm, s + 1)
                            need(dve, exp_done, s - 1)
                            carry_waits(j)
                            for h in range(HEADS):
                                cols = slice(h * N, (h + 1) * N)
                                op = dve.tensor_tensor_reduce(scores[:, j % 2, cols], (S0, S1)[j % 2][:, cols], mask[:],
                                                              -1.0, 3.0e38, ALU.add, ALU.min,
                                                              neg_max[:, j % 2, h:h + 1])
                            op.then_inc(score_max, 1)
                        if t.has(A if j >= 1 else L):
                            need(dve, pt_mm, s)
                            need(dve, av_mm, s - 2)
                            dve.tensor_copy(probs_t[:, (j + 1) % 2, :], PTB[:]).then_inc(pt_out, 1)
                        if t.has(P) and j == 1:
                            need(dve, k_mm, t.group(P) + 1)
                            need(dve, score_mm, (t.group(P) - 1) * GB)
                            dve.tensor_copy(k_t[:, t.par(P), :], R1[:]).then_inc(k_out, 1)
                        if t.has(P) and j == 2:
                            need(dve, v_mm, t.group(P) + 1)
                            need(dve, av_mm, (t.group(P) - 1) * GB)
                            dve.tensor_copy(
                                v_one[:, t.par(P), :, :].rearrange("p b (h v) -> p (b h) v", v=VW)[:, :, 0:HD],
                                R0[:].rearrange("p (c v) -> p c v", v=HD)).then_inc(v_out, 1)
                        lag = A if j >= 2 else L
                        if t.has(lag):
                            o = OB[:, 0:HEADS * VW].rearrange("p (h v) -> p h v", v=VW)
                            need(dve, av_mm, s - 1)
                            dve.reciprocal(recip, o[:, :, HD]).then_inc(av_recip, 1)
                            need(dve, av_recip, s - 1)
                            b = (j - 2) % GB
                            if b == 0:
                                need(dve, s0_done, t.group(lag) - 1)
                            dve.tensor_tensor(
                                attn[:, t.par(lag), b * D:(b + 1) * D].rearrange("p (h v) -> p h v", v=HD),
                                o[:, :, 0:HD], recip.unsqueeze(2).broadcast_to([N, HEADS, HD]),
                                ALU.mult).then_inc(av_out, 1)
                        if t.has(H) and j == 0:
                            need(dve, z_mm, (t.group(H) + 1) * GB)
                            need(dve, x1b_done, t.group(H) + 1)
                            dve.tensor_tensor(s1, ZB[:], x1b[:, t.par(H), :], ALU.add).then_inc(s1_done, 1)
                            need(dve, s1_done, t.group(H) + 1)
                            need(dve, ve1, t.group(H))
                            ln_stats(1, s1, st1, mv1, t.group(H))
                        if t.has(H) and j == 1:
                            need(dve, rs1, t.group(H) + 1)
                            need(dve, g_mm, t.group(H))
                            need(dve, x2_kept, t.group(H))
                            ln_apply(1, s1, x2, x2_done)
                        if t.has(L) and j == 2:
                            need(dve, s0_done, t.group(L) + 1)
                            ln_stats(0, s0, st0, mv0, t.group(L))
                        if t.has(L) and j == 3:
                            need(dve, rs0, t.group(L) + 1)
                            need(dve, y_mm, (t.group(L) - 1) * GB)
                            need(dve, x1b_done, t.group(L) - 1)
                            ln_apply(0, s0, x1[:, t.par(L), :], x1_done)
                        if t.has(H) and j == 3:
                            for k in range(HID):
                                need(dve, h_out, t.group(H) * HID + k + 1)
                                dve.bn_stats(bn_stats1[:, k, ds(t.group(H), 1), :].rearrange("p a s -> p (a s)"),
                                             wide[:, k, ds(t.group(H) * T, T)]).then_inc(h_stat, 1)

                turns(dve, turn, -1, 4, G - 2, G + 3)

            @block.gpsimd
            def _(pool):
                def rstd(i, mv_sem, eps_sem, done, group):
                    need(pool, mv_sem, (group + 1) * GB)
                    pool.tensor_tensor(ln_rs[:, i, :], ln_mv[:, i, :, 1], eps_tile, ALU.add).then_inc(eps_sem, 1)
                    need(pool, eps_sem, group + 1)
                    pool.tensor_tensor(ln_rs[:, i, :], ln_rs[:, i, :], neg_half, ALU.pow).then_inc(done, 1)

                def turn(t):
                    if t.has(H):
                        need(pool, x2_done, t.group(H))
                        rstd(1, mv1, ve1, rs1, t.group(H))
                    if t.has(L):
                        need(pool, av_out, (t.group(L) + 1) * GB)
                        need(pool, xg_ld[t.par(L)], (t.half(L) + 1) * 16)
                        need(pool, x1_done, t.group(L))
                        pool.tensor_tensor(s0, attn[:, t.par(L), :], xg[:, t.par(L), :], ALU.add).then_inc(s0_done, 1)
                    if t.has(H):
                        need(pool, x2_done, t.group(H) + 1)
                        pool.tensor_copy(xres[:, ds(t.group(H) * GB, GB), :].rearrange("p b d -> p (b d)"),
                                         x2).then_inc(x2_kept, 1)
                    if t.has(L):
                        rstd(0, mv0, ve0, rs0, t.group(L))
                        need(pool, x1_done, t.group(L) + 1)
                        need(pool, s1_done, t.group(L) - 1)
                        pool.tensor_tensor(x1b[:, t.par(L), :].rearrange("p (b d) -> p b d", d=D),
                                           x1[:, t.par(L), :].rearrange("p (b d) -> p b d", d=D),
                                           row_bias[:, 0:1, :].broadcast_to([N, GB, D]),
                                           ALU.add).then_inc(x1b_done, 1)

                turns(pool, turn, 0, 4, G, G + 3)

        spot[0] = 0
        hid = carve(2, HID, T)
        bn_pool, bn_dve = sem("bn_pool"), sem("bn_dve")
        relu_done, mlp_mm, y2_out, y2_stat = sem("relu_done"), sem("mlp_mm"), sem("y2_out"), sem("y2_stat")

        def bn_finish_dve(dve, slot, stats, gain, offset, dve_at, pool_at):
            f = bn_fin[:, slot, :]
            dve.bn_aggr(f[:, 0:2], stats).then_inc(bn_dve, 1)
            dve.wait_ge(bn_pool, pool_at + 2)
            dve.tensor_tensor(f[:, 4:5], f[:, 3:4], gain, ALU.mult).then_inc(bn_dve, 1)
            dve.wait_ge(bn_dve, dve_at + 2)
            dve.scalar_tensor_tensor(bn_tmp[:, slot:slot + 1], f[:, 0:1], -1.0, f[:, 4:5],
                                     ALU.mult, ALU.mult).then_inc(bn_dve, 1)
            dve.wait_ge(bn_dve, dve_at + 3)
            dve.tensor_tensor(f[:, 5:6], bn_tmp[:, slot:slot + 1], offset, ALU.add).then_inc(bn_dve, 1)

        def bn_finish_pool(pool, slot, dve_at, pool_at):
            f = bn_fin[:, slot, :]
            pool.wait_ge(bn_dve, dve_at + 1)
            pool.tensor_tensor(f[:, 2:3], f[:, 1:2], eps_tile[:, 0:1], ALU.add).then_inc(bn_pool, 1)
            pool.wait_ge(bn_pool, pool_at + 1)
            pool.tensor_tensor(f[:, 3:4], f[:, 2:3], neg_half[:, 0:1], ALU.pow).then_inc(bn_pool, 1)

        with nc.Block() as block:
            @block.vector
            def _(dve):
                for k in range(HID):
                    bn_finish_dve(dve, k, bn_stats1[:, k, :, :].rearrange("p g s -> p (g s)"),
                                  bn1p[:, 1, k:k + 1], bn1p[:, 2, k:k + 1], 4 * k, 2 * k)

                def turn(t):
                    g = t.group(0)
                    cols = ds(g * T, T)
                    need(dve, mlp_mm, g + 1)
                    dve.tensor_scalar(wide[:, 0, cols], bank[t.par(0)][:], bn2p[:, 0:1], None, ALU.add) \
                       .then_inc(y2_out, 1)
                    need(dve, y2_out, g + 1)
                    dve.bn_stats(bn_stats2[:, ds(g, 1), :].rearrange("p a s -> p (a s)"), wide[:, 0, cols]) \
                       .then_inc(y2_stat, 1)

                turns(dve, turn, 0, 2, G, G)

            @block.gpsimd
            def _(pool):
                for k in range(HID):
                    bn_finish_pool(pool, k, 4 * k, 2 * k)

            @block.scalar
            def _(act):
                act.wait_ge(bn_dve, 4 * HID)

                def turn(t):
                    g = t.group(0)
                    need(act, mlp_mm, g - 1)
                    for k in range(HID):
                        act.activation(hid[:, t.par(0), k, :], wide[:, k, ds(g * T, T)], ACT.Relu,
                                       bias=bn_fin[:, k, 5:6], scale=bn_fin[:, k, 4:5]).then_inc(relu_done, 1)

                turns(act, turn, 0, 2, G, G)

            @block.tensor
            def _(pe):
                def turn(t):
                    g = t.group(0)
                    need(pe, y2_out, g - 1)
                    for k in range(HID):
                        need(pe, relu_done, g * HID + k + 1)
                        mm = pe.matmul(bank[t.par(0)][:], w2t[:, k, :], hid[:, t.par(0), k, :],
                                       start=(k == 0), stop=(k == HID - 1))
                    mm.then_inc(mlp_mm, 1)

                turns(pe, turn, 0, 2, G, G)

        spot[0] = 0
        y_bn = carve(2, T)
        s2 = carve(T)
        x3 = carve(2, T)
        x3_t = carve(T)
        u0 = carve(T)
        v0 = carve(T)
        u1 = carve(T)
        ln2_st = carve(GB, 6)
        ln2_mv = carve(GB, 2)
        ln2_ve = carve(GB)
        ln2_rs = carve(GB)
        BT, XT, U0, V0, U1, V1 = bank[0:6]
        ybn_done, bt_mm, s2_done, st2, mv2, ve2, rs2 = (
            sem("ybn_done"), sem("bt_mm"), sem("s2_done"), sem("st2"), sem("mv2"), sem("ve2"), sem("rs2"))
        x3_done, x3_kept, xt_mm, xt_out = sem("x3_done"), sem("x3_kept"), sem("xt_mm"), sem("xt_out")
        u0_mm, u0_out, v0_mm, v0_out = sem("u0_mm"), sem("u0_out"), sem("v0_mm"), sem("v0_out")
        u1_mm, u1_out, v1_mm, v1_out = sem("u1_mm"), sem("u1_out"), sem("v1_mm"), sem("v1_out")

        def by_batch(a):
            return a.rearrange("p (b d) -> p b d", d=D)

        with nc.Block() as block:
            @block.tensor
            def _(pe):
                def four(out, lhs, rhs, done):
                    for b in range(GB):
                        cols = slice(b * 128, (b + 1) * 128)
                        if rhs is None:
                            mm = pe.transpose(out[:, cols], lhs[:, cols], ident[:])
                        else:
                            mm = pe.matmul(out[:, cols], lhs[:, cols], rhs, start=True, stop=True)
                    mm.then_inc(done, 1)

                def turn(t):
                    if t.has(2):
                        need(pe, u0_out, t.group(2) + 1)
                        need(pe, v0_out, t.group(2))
                        four(V0, u0, adjt[:], v0_mm)
                    if t.has(1):
                        need(pe, x3_done, t.group(1) + 1)
                        need(pe, xt_out, t.group(1))
                        four(XT, x3[:, t.par(1), :], None, xt_mm)
                    if t.has(0):
                        need(pe, ybn_done, t.group(0) + 1)
                        need(pe, s2_done, t.group(0))
                        four(BT, y_bn[:, t.par(0), :], None, bt_mm)
                    if t.has(2):
                        need(pe, v0_out, t.group(2) + 1)
                        need(pe, u1_out, t.group(2))
                        four(U1, v0, wg[:, 1, :], u1_mm)
                    if t.has(1):
                        need(pe, xt_out, t.group(1) + 1)
                        need(pe, u0_out, t.group(1))
                        four(U0, x3_t, wg[:, 0, :], u0_mm)
                    if t.has(2):
                        need(pe, u1_out, t.group(2) + 1)
                        need(pe, v1_out, t.group(2))
                        four(V1, u1, adjt[:], v1_mm)

                turns(pe, turn, 0, 4, G, G + 2)

            @block.scalar
            def _(act):
                act.wait_ge(bn_dve, 4 * (HID + 1))

                def turn(t):
                    if t.has(2):
                        need(act, v0_mm, t.group(2) + 1)
                        need(act, u1_mm, t.group(2))
                        act.activation(v0, V0[:], ACT.Relu).then_inc(v0_out, 1)
                    if t.has(1):
                        need(act, xt_mm, t.group(1) + 1)
                        need(act, u0_mm, t.group(1))
                        act.copy(x3_t, XT[:]).then_inc(xt_out, 1)
                    if t.has(-1):
                        need(act, bt_mm, t.group(-1) - 1)
                        act.activation(y_bn[:, t.par(-1), :], wide[:, 0, ds(t.group(-1) * T, T)], ACT.Identity,
                                       bias=bn_fin[:, HID, 5:6], scale=bn_fin[:, HID, 4:5]).then_inc(ybn_done, 1)
                    if t.has(2):
                        need(act, v1_mm, t.group(2) + 1)
                        act.activation(wide[:, 1, ds(t.group(2) * T, T)], V1[:], ACT.Relu).then_inc(v1_out, 1)

                turns(act, turn, -1, 3, G - 1, G + 2)

            @block.vector
            def _(dve):
                bn_finish_dve(dve, HID, bn_stats2[:].rearrange("p g s -> p (g s)"), bn2p[:, 1:2], bn2p[:, 2:3],
                              4 * HID, 2 * HID)

                def turn(t):
                    if t.has(0):
                        g = t.group(0)
                        need(dve, bt_mm, g + 1)
                        dve.tensor_tensor(by_batch(s2), by_batch(BT[:]), xres[:, ds(g * GB, GB), :],
                                          ALU.add).then_inc(s2_done, 1)
                        need(dve, s2_done, g + 1)
                        for b in range(GB):
                            dve.bn_stats(ln2_st[:, b, :], s2[:, b * D:(b + 1) * D]).then_inc(st2, 1)
                    if t.has(2):
                        need(dve, u1_mm, t.group(2) + 1)
                        need(dve, v1_mm, t.group(2))
                        dve.tensor_tensor(by_batch(u1), by_batch(U1[:]), row_bias[:, 2:3, :].broadcast_to([N, GB, D]),
                                          ALU.add).then_inc(u1_out, 1)
                    if t.has(0):
                        need(dve, st2, (t.group(0) + 1) * GB)
                        dve.memset(idle_words[:, t.par(0):t.par(0) + 1], 0.0)
                        for b in range(GB):
                            dve.bn_aggr(ln2_mv[:, b, :], ln2_st[:, b, :]).then_inc(mv2, 1)
                    if t.has(1):
                        need(dve, u0_mm, t.group(1) + 1)
                        need(dve, v0_mm, t.group(1))
                        dve.tensor_tensor(by_batch(u0), by_batch(U0[:]), row_bias[:, 1:2, :].broadcast_to([N, GB, D]),
                                          ALU.add).then_inc(u0_out, 1)
                    if t.has(0):
                        need(dve, rs2, t.group(0) + 1)
                        need(dve, xt_mm, t.group(0) - 1)
                        need(dve, x3_kept, t.group(0) - 1)
                        for b in range(GB):
                            op = dve.tensor_scalar(x3[:, t.par(0), b * D:(b + 1) * D], s2[:, b * D:(b + 1) * D],
                                                   ln2_mv[:, b, 0:1], ln2_rs[:, b:b + 1], ALU.subtract, ALU.mult)
                        op.then_inc(x3_done, 1)

                turns(dve, turn, 0, 4, G, G + 2)

            @block.gpsimd
            def _(pool):
                bn_finish_pool(pool, HID, 4 * HID, 2 * HID)

                def turn(t):
                    g = t.group(0)
                    need(pool, mv2, (g + 1) * GB)
                    pool.tensor_tensor(ln2_ve, ln2_mv[:, :, 1], eps_tile, ALU.add).then_inc(ve2, 1)
                    need(pool, ve2, g + 1)
                    pool.tensor_tensor(ln2_rs, ln2_ve, neg_half, ALU.pow).then_inc(rs2, 1)
                    need(pool, x3_done, g + 1)
                    pool.tensor_copy(xres[:, ds(g * GB, GB), :], by_batch(x3[:, t.par(0), :])).then_inc(x3_kept, 1)

                turns(pool, turn, 0, 2, G, G)

        spot[0] = 0
        SB = 8
        ROUNDS = B // (2 * SB)
        ST = SB * N
        C = 512
        I_, F_, G_, O_ = range(GATES)
        hs = [carve(SB, N) for _ in range(2)]
        act_i, act_f, act_g, act_o, cell, tanh_c, h_mid, fc = (
            [carve(C) for _ in range(2)] for _ in range(8))
        s3 = [carve(ST) for _ in range(2)]
        fin = [carve(ST) for _ in range(2)]
        ln3_st = [carve(SB, 6) for _ in range(2)]
        ln3_mv = [carve(SB, 2) for _ in range(2)]
        ln3_ve = [carve(SB) for _ in range(2)]
        ln3_rs = [carve(SB) for _ in range(2)]

        def pair(name):
            return [sem(f"{name}{a}") for a in range(2)]

        hs_ld, gate_mm, gate_out, cell_ops, cell_done, tanh_done, h_done = map(pair, (
            "hs_ld", "gate_mm", "gate_out", "cell_ops", "cell_done", "tanh_done", "h_done"))
        back_mm, s3_done, st3, mv3, ve3, rs3, fin_done, fin_st = map(pair, (
            "back_mm", "s3_done", "st3", "mv3", "ve3", "rs3", "fin_done", "fin_st"))

        class Step:
            pass

        steps = []
        gates_before = cells_before = 0
        for p in range(1, STEPS + 1):
            windows = N // p
            for part in range(2 if p == 1 else 1):
                for t in range(p):
                    st = Step()
                    st.p, st.t, st.first, st.last = p, t, t == 0, t == p - 1
                    st.gates = (I_, G_, O_) if st.first else (I_, G_, F_, O_)
                    st.b0, st.nb = (part * SB // 2, SB // 2) if p == 1 else (0, SB)
                    st.nodes = slice(t, t + (windows - 1) * p + 1, p)
                    st.windows, st.cols = windows, st.nb * windows
                    st.n = len(steps)
                    st.mids = sum(1 for s in steps if not s.first)
                    st.pass_start = sum(1 for s in steps if s.p < p)
                    st.gates_before, st.cells_before = gates_before, cells_before
                    gates_before += len(st.gates)
                    cells_before += 1 if st.first else 3
                    assert st.cols <= C
                    steps.append(st)
        NS, GATES_ROUND, CELLS_ROUND = len(steps), gates_before, cells_before

        def nodes_of(a, st):
            return hs[a][:, st.b0:st.b0 + st.nb, st.nodes]

        def flat(tile, st):
            return tile[:, 0:st.cols].rearrange("p (b w) -> p b w", w=st.windows)

        with nc.Block() as block:
            @block.gpsimd
            def _(pool):
                def load(a, lg):
                    pool.tensor_copy(hs[a].rearrange("p b n -> p (b n)"), wide[:, 1, ds(lg * ST, ST)]) \
                        .then_inc(hs_ld[a], 1)

                def norm(a, r):
                    need(pool, mv3[a], (r + 1) * SB)
                    pool.tensor_tensor(ln3_ve[a], ln3_mv[a][:, :, 1], eps_wide[:], ALU.add).then_inc(ve3[a], 1)
                    need(pool, ve3[a], r + 1)
                    pool.tensor_tensor(ln3_rs[a], ln3_ve[a], neg_half_wide[:], ALU.pow).then_inc(rs3[a], 1)

                for a in range(2):
                    load(a, a)
                with pool.Fori(0, ROUNDS - 1) as r:
                    for a in range(2):
                        need(pool, s3_done[a], (r + 1) * 2)
                        load(a, (r + 1) * 2 + a)
                    for a in range(2):
                        norm(a, r)
                for a in range(2):
                    norm(a, ROUNDS - 1)

            @block.tensor
            def _(pe):
                with pe.Fori(0, ROUNDS) as r:
                    for st in steps:
                        for a in range(2):
                            out = [flat(bank[4 * a + gate], st) for gate in range(GATES)]
                            if st.n == 0:
                                need(pe, hs_ld[a], r + 1)
                            else:
                                need(pe, gate_out[a], r * GATES_ROUND + st.gates_before)
                            if st.first and st.pass_start:
                                need(pe, h_done[a], r * NS + st.pass_start)
                            for gate in st.gates:
                                mm = pe.matmul(out[gate], wiht[:, st.p - 1, gate * D:(gate + 1) * D], nodes_of(a, st),
                                               start=True, stop=st.first)
                                if st.first:
                                    mm.then_inc(gate_mm[a], 1)
                            if not st.first:
                                need(pe, h_done[a], r * NS + st.n)
                                for gate in st.gates:
                                    pe.matmul(out[gate], whht[:, st.p - 1, gate * D:(gate + 1) * D],
                                              flat(h_mid[a], st), start=False, stop=True).then_inc(gate_mm[a], 1)
                    for a in range(2):
                        need(pe, h_done[a], (r + 1) * NS)
                        for half in range(2):
                            for b in range(GB):
                                mm = pe.transpose(bank[4 * a + half][:, b * D:(b + 1) * D],
                                                  hs[a][:, half * GB + b, :], ident[:])
                            mm.then_inc(back_mm[a], 1)

            @block.scalar
            def _(act):
                tiles = {I_: act_i, F_: act_f, G_: act_g, O_: act_o}
                with act.Fori(0, ROUNDS) as r:
                    for st in steps:
                        for a in range(2):
                            for k, gate in enumerate(st.gates):
                                need(act, gate_mm[a], r * GATES_ROUND + st.gates_before + k + 1)
                                if k == 0 and st.n:
                                    need(act, h_done[a], r * NS + st.n)
                                at = (st.p - 1) * GATES + gate
                                act.activation(tiles[gate][a][:, 0:st.cols], bank[4 * a + gate][:, 0:st.cols],
                                               ACT.Tanh if gate == G_ else ACT.Sigmoid,
                                               bias=gate_bias[:, at:at + 1]).then_inc(gate_out[a], 1)
                            need(act, cell_done[a], r * NS + st.n + 1)
                            act.activation(tanh_c[a][:, 0:st.cols], cell[a][:, 0:st.cols], ACT.Tanh) \
                               .then_inc(tanh_done[a], 1)

            @block.vector
            def _(dve):
                with dve.Fori(0, ROUNDS) as r:
                    for st in steps:
                        for a in range(2):
                            c = slice(0, st.cols)
                            gates = r * GATES_ROUND + st.gates_before
                            if st.first:
                                need(dve, gate_out[a], gates + 2)
                                dve.tensor_tensor(cell[a][:, c], act_i[a][:, c], act_g[a][:, c], ALU.mult) \
                                   .then_inc(cell_done[a], 1)
                            else:
                                mine = r * 2 * (NS - STEPS - 1) + 2 * st.mids
                                need(dve, gate_out[a], gates + 2)
                                dve.tensor_tensor(act_i[a][:, c], act_i[a][:, c], act_g[a][:, c], ALU.mult) \
                                   .then_inc(cell_ops[a], 1)
                                need(dve, gate_out[a], gates + 3)
                                dve.tensor_tensor(fc[a][:, c], act_f[a][:, c], cell[a][:, c], ALU.mult) \
                                   .then_inc(cell_ops[a], 1)
                                need(dve, cell_ops[a], mine + 2)
                                dve.tensor_tensor(cell[a][:, c], act_i[a][:, c], fc[a][:, c], ALU.add) \
                                   .then_inc(cell_done[a], 1)
                            need(dve, tanh_done[a], r * NS + st.n + 1)
                            if st.last:
                                out = nodes_of(a, st)
                            else:
                                out = flat(h_mid[a], st)
                            dve.tensor_tensor(out, flat(act_o[a], st), flat(tanh_c[a], st), ALU.mult) \
                               .then_inc(h_done[a], 1)
                    for a in range(2):
                        lg = r * 2 + a
                        for half in range(2):
                            need(dve, back_mm[a], r * 2 + half + 1)
                            dve.tensor_tensor(by_batch(s3[a][:, half * T:(half + 1) * T]),
                                              by_batch(bank[4 * a + half][:]),
                                              xres[:, ds(lg * SB + half * GB, GB), :], ALU.add) \
                               .then_inc(s3_done[a], 1)
                        need(dve, s3_done[a], r * 2 + 2)
                        for b in range(SB):
                            dve.bn_stats(ln3_st[a][:, b, :], s3[a][:, b * D:(b + 1) * D]).then_inc(st3[a], 1)
                        need(dve, st3[a], (r + 1) * SB)
                        dve.memset(idle_words[:, a:a + 1], 0.0)
                        for b in range(SB):
                            dve.bn_aggr(ln3_mv[a][:, b, :], ln3_st[a][:, b, :]).then_inc(mv3[a], 1)
                    for a in range(2):
                        need(dve, fin_st[a], r * 16 + 16)
                        need(dve, rs3[a], r + 1)
                        for b in range(SB):
                            op = dve.tensor_scalar(fin[a][:, b * D:(b + 1) * D], s3[a][:, b * D:(b + 1) * D],
                                                   ln3_mv[a][:, b, 0:1], ln3_rs[a][:, b:b + 1],
                                                   ALU.subtract, ALU.mult)
                        op.then_inc(fin_done[a], 1)

            @block.sync
            def _(sp):
                for a in range(2):
                    sp.sem_inc(fin_st[a], 16)
                with sp.Fori(0, ROUNDS) as r:
                    for a in range(2):
                        need(sp, fin_done[a], r + 1)
                        sp.dma_start(io["out"][:, ds((r * 2 + a) * ST, ST)], fin[a]).then_inc(fin_st[a], 16)
                for a in range(2):
                    sp.wait_ge(fin_st[a], 16 * (ROUNDS + 1))


_DRAM = (("x", (N, B * D)), ("xt", (D, TOKENS)), ("adj", (N, N)), ("adjt", (N, N)), ("wqkv", (D, 3 * D)),
         ("w_l1", (D, 3, D)), ("rows", (1, 3, D)), ("w1t", (D, HID * 128)), ("w2t", (128, HID, D)),
         ("wg", (D, 2, D)), ("wiht", (D, STEPS, GATES * D)), ("whht", (D, STEPS, GATES * D)),
         ("bn1p", (128, 3, HID)), ("bn2p", (128, 3)), ("lstm_b", (D, 2, STEPS * GATES)))


def kernel(**inputs):
    import numpy as np
    import concourse.bacc as bacc
    from concourse.bass_utils import run_bass_kernel_spmd

    a = {k: np.asarray(v) for k, v in inputs.items()}
    cols = lambda v: v.reshape(-1, 128).T
    gates_t = lambda w: w.transpose(2, 0, 1)
    laid = {
        "x": a["x"].transpose(1, 0, 2).reshape(N, B * D),
        "xt": a["x"].transpose(2, 0, 1).reshape(D, TOKENS),
        "adj": a["adj"], "adjt": a["adj"].T, "wqkv": a["L0_gnn_W"],
        "w_l1": a["L1_gnn_W"].transpose(1, 0, 2),
        "rows": np.stack([a["L1_gnn_bias"], a["L3_gnn_bg0"], a["L3_gnn_bg1"]])[None],
        "w1t": a["L2_gnn_W1"].T,
        "w2t": a["L2_gnn_W2"].T.reshape(HID, 128, D).transpose(1, 0, 2),
        "wg": np.stack([a["L3_gnn_Wg0"], a["L3_gnn_Wg1"]], axis=1),
        "wiht": gates_t(a["L3_gnn_Wih"]), "whht": gates_t(a["L3_gnn_Whh"]),
        "bn1p": np.stack([cols(a[f"L2_gnn_{n}"]) for n in ("b1", "g1", "be1")], axis=1),
        "bn2p": np.concatenate([cols(a[f"L2_gnn_{n}"]) for n in ("b2", "g2", "be2")], axis=1),
        "lstm_b": np.stack([cols(a["L3_gnn_bih"].reshape(-1)), cols(a["L3_gnn_bhh"].reshape(-1))], axis=1),
    }
    laid = {k: np.ascontiguousarray(v) for k, v in laid.items()}

    nc = bacc.Bacc("TRN2", target_bir_lowering=False, num_devices=1)
    io = {n: nc.dram_tensor(f"in_{n}", s, F32, kind="ExternalInput").ap() for n, s in _DRAM}
    io["out"] = nc.dram_tensor("out", (N, B * D), F32, kind="ExternalOutput").ap()
    build(nc, io)
    r = run_bass_kernel_spmd(nc, [{f"in_{n}": v for n, v in laid.items()}], core_ids=[0])
    return np.ascontiguousarray(r.results[0]["out"].reshape(N, B, D).transpose(1, 0, 2))
```

```python
from contextlib import ExitStack

import concourse.bass as bass
from concourse import mybir

F32 = mybir.dt.float32
F32R = mybir.dt.float32r
ALU = mybir.AluOpType
ACT = mybir.ActivationFunctionType
AX_X = mybir.AxisListType.X

B, N, D = 64, 128, 128
HEADS = 4
HD = D // HEADS
VW = HD + 2
GB = 4
G = B // GB
T = GB * N
TOKENS = B * N
HID = 2
STEPS = 4
GATES = 4
EPS = 1e-5
WORK_A = 16664
WORK_B = 2 * HID * T
WORK_C = 5760
MASKED = -1.0e30



def ds(start, size):
    return bass.ds(start, size)


def need(eng, sem, value):
    if isinstance(value, int) and value <= 0:
        return
    eng.wait_ge(sem, value)


class Turn:

    def __init__(self, m, c, peeled):
        self.m, self.c, self.peeled = m, c, peeled

    def group(self, lag):
        return self.m * 2 + (self.c - lag)

    def half(self, lag):
        return self.m + (self.c - lag) // 2

    def par(self, lag):
        return (self.c - lag) % 2

    def has(self, lag, count=G):
        return not self.peeled or 0 <= self.c - lag < count


def turns(eng, body, first, steady, steady_end, last):
    for c in range(first, steady):
        body(Turn(0, c, True))
    with eng.Fori(0, (steady_end - steady) // 2) as m:
        for u in range(2):
            body(Turn(m, steady + u, False))
    for c in range(steady_end, last):
        body(Turn(0, c, True))


def build(nc, io):
    with ExitStack() as ctx:
        def sb(name, shape, dt=F32, side=None, scope=ctx):
            return scope.enter_context(nc.sbuf_tensor(name, shape, dt, side=side))

        def sem(name):
            return ctx.enter_context(nc.semaphore(name))

        bank = [ctx.enter_context(nc.psum_tensor(f"bank{i}", [128, 512], F32)) for i in range(8)]

        hidden = ctx.enter_context(ExitStack())
        wide0 = sb("wide0", [128, TOKENS], side="right", scope=hidden)
        early = ctx.enter_context(ExitStack())
        wide1 = sb("wide1", [128, TOKENS], side="right", scope=early)
        wqkv = sb("wqkv", [D, 3 * D], side="right", scope=early)
        w_l1 = sb("w_l1", [D, 3, D], side="right", scope=early)
        w1t = sb("w1t", [D, HID * 128], side="right", scope=early)
        w2t = sb("w2t", [128, HID, D], side="right", scope=early)
        wg = sb("wg", [D, 2, D])
       
        adj = sb("adj", [N, N], side="right", scope=early)
        adjt = sb("adjt", [N, N])
        bn1p = sb("bn1p", [128, 3, HID])
        bn2p = sb("bn2p", [128, 3])
        lstm_b = sb("lstm_b", [D, 2, STEPS * GATES])
        gate_bias = sb("gate_bias", [D, STEPS * GATES])
        rows = sb("rows", [1, 3, D])
        row_bias = sb("row_bias", [128, 3, D])
        ident = sb("ident", [128, 128])
        ones_row = sb("ones_row", [1, 128])
        eps_wide = sb("eps_wide", [128, 2 * GB])
        neg_half_wide = sb("neg_half_wide", [128, 2 * GB])
        eps_tile, neg_half = eps_wide[:, 0:GB], neg_half_wide[:, 0:GB]
        zero_wide = sb("zero_wide", [128, 2 * GB])
        bn_tmp = sb("bn_tmp", [128, HID + 1])
        idle_words = sb("idle_words", [128, 8])
        mask = sb("mask", [N, N], side="right", scope=early)
        adj_split_t = sb("adj_split_t", [N, 3, N], side="right", scope=early)
        ahat_t = sb("ahat_t", [N, N], side="right", scope=early)
        anorm = sb("anorm", [N, N], side="right", scope=early)
        anorm_t = sb("anorm_t", [N, N], side="right", scope=early)
        degs = sb("degs", [N, 8])
        bn_stats1 = sb("bn_stats1", [128, HID, G, 6])
        bn_stats2 = sb("bn_stats2", [128, G, 6])
        bn_fin = sb("bn_fin", [128, 3, 6])

        xres = sb("xres", [N, B, D])
        wide = (wide0, wide1)

        work_a = ctx.enter_context(ExitStack())
        work = sb("work_a", [128, WORK_A], side="right", scope=work_a)
        spot = [0]

        def carve(*shape):
            n = 1
            for s in shape:
                n *= s
            a = work[:, spot[0]:spot[0] + n]
            spot[0] += n
            assert spot[0] <= work.shape[1], spot
            if len(shape) == 2:
                a = a.rearrange("p (a b) -> p a b", b=shape[1])
            elif len(shape) == 3:
                a = a.rearrange("p (a b c) -> p a b c", b=shape[1], c=shape[2])
            return a

        xt_in = carve(2, T)
        xg = carve(2, T)
        q_all = carve(T)
        q_head = carve(2, HEADS, T)
        k_t = carve(2, T)
        v_one = carve(2, GB, HEADS * VW)
        scores = carve(2, HEADS * N)
        neg_max = carve(2, HEADS)
        probs = carve(2, HEADS * N)
        probs_t = carve(2, HEADS * N)
        recip = carve(HEADS)
        attn = carve(2, T)
        x1 = carve(2, T)
        agg3 = carve(2, 3 * N)
        s1 = carve(T)
        x2 = carve(T)
        agg_t = carve(T)
        ln_st = carve(2, GB, 6)
        ln_mv = carve(2, GB, 2)
        ln_rs = carve(2, GB)

        def halves(name, shape):
            return [sb(f"{name}_{part}", shape, F32R, side="right", scope=work_a) for part in ("hi", "lo")]

        xt_hi, xt_lo = halves("xt", [D, 2, T])
        x1_hi, x1_lo = halves("x1", [N, 2, T])
        agg_hi, agg_lo = halves("agg", [D, T])
        wqk_hi, wqk_lo = halves("wqk", [D, 2 * D])
        w1t_hi, w1t_lo = halves("w1t", [D, HID * 128])
        adj3_hi, adj3_lo = halves("adj3", [N, 3 * N])
        xt_hi_done, xt_lo_done, x1_hi_done, x1_lo_done, g_lo, qk_split, late_split = map(sem, (
            "xt_hi_done", "xt_lo_done", "x1_hi_done", "x1_lo_done", "g_lo", "qk_split", "late_split"))

        xt_ld = [sem(f"xt_ld{i}") for i in range(2)]
        xg_ld = [sem(f"xg_ld{i}") for i in range(2)]
        qh_ld = [sem(f"qh_ld{i}") for i in range(2)]
        bufs_set = sem("bufs_set")
        adj_loaded, wqkv_loaded, rows_loaded, w_l1_loaded, mlp1_loaded, rest_loaded = map(sem, (
            "adj_loaded", "wqkv_loaded", "rows_loaded", "w_l1_loaded", "mlp1_loaded", "rest_loaded"))
        REST_LOADS = 4
        pool_setup = sem("pool_setup")
        dve_setup = sem("dve_setup")
        pe_setup = sem("pe_setup")

        with nc.Block() as block:
            @block.sync
            def _(sp):
                sp.dma_start(adj[:], io["adj"]).then_inc(adj_loaded, 16)
                sp.dma_start(adjt[:], io["adjt"]).then_inc(adj_loaded, 16)
                sp.dma_start(wqkv[:], io["wqkv"]).then_inc(wqkv_loaded, 16)
                sp.dma_start(xt_in[:, 0, :], io["xt"][:, 0:T]).then_inc(xt_ld[0], 16)
                sp.dma_start(rows[:], io["rows"]).then_inc(rows_loaded, 16)
                sp.dma_start(xt_in[:, 1, :], io["xt"][:, T:2 * T]).then_inc(xt_ld[1], 16)
                for g in range(2):
                    sp.dma_start(xg[:, g, :], io["x"][:, g * T:(g + 1) * T]).then_inc(xg_ld[g], 16)
                sp.dma_start(w_l1[:], io["w_l1"]).then_inc(w_l1_loaded, 16)
                for tile, name in ((w1t, "w1t"), (bn1p, "bn1p")):
                    sp.dma_start(tile[:], io[name]).then_inc(mlp1_loaded, 16)
                for tile, name in ((w2t, "w2t"), (bn2p, "bn2p"), (wg, "wg"), (lstm_b, "lstm_b")):
                    sp.dma_start(tile[:], io[name]).then_inc(rest_loaded, 16)

            @block.gpsimd
            def _(pool):
                pool.memset(ident[:], 0.0).then_inc(pool_setup, 1)
                pool.memset(ones_row[:], 1.0).then_inc(pool_setup, 1)
                pool.memset(neg_half_wide[:], -0.5).then_inc(pool_setup, 1)
                pool.memset(eps_wide[:], EPS).then_inc(pool_setup, 1)
                pool.memset(zero_wide[:], 0.0).then_inc(pool_setup, 1)
                pool.wait_ge(pool_setup, 5)
                pool.affine_select(out=ident[:], in_=ident[:], compare_op=ALU.not_equal, fill=1.0, base=0,
                                   pattern=[[-1, N]], channel_multiplier=1).then_inc(pool_setup, 1)
                pool.memset(q_head[:, 1].rearrange("p h t -> p (h t)"), 0.0).then_inc(bufs_set, 1)
                pool.wait_ge(adj_loaded, 32)
                pool.affine_select(out=adj_split_t[:, 0, :], in_=adjt[:], compare_op=ALU.is_equal, fill=0.0,
                                   base=0, pattern=[[-1, N]], channel_multiplier=1).then_inc(pool_setup, 1)
                pool.affine_select(out=adj_split_t[:, 1, :], in_=adjt[:], compare_op=ALU.is_gt, fill=0.0,
                                   base=0, pattern=[[-1, N]], channel_multiplier=1).then_inc(pool_setup, 1)
                pool.affine_select(out=adj_split_t[:, 2, :], in_=adjt[:], compare_op=ALU.is_gt, fill=0.0,
                                   base=0, pattern=[[1, N]], channel_multiplier=-1).then_inc(pool_setup, 1)
                pool.wait_ge(dve_setup, 8)
                pool.tensor_tensor(degs[:, 5:6], degs[:, 4:5], neg_half[:, 0:1], ALU.pow).then_inc(pool_setup, 1)

            @block.vector
            def _(dve):
                dve.memset(q_head[:, 0].rearrange("p h t -> p (h t)"), 0.0).then_inc(bufs_set, 1)
                dve.memset(v_one.rearrange("p a b v -> p (a b v)"), 1.0).then_inc(bufs_set, 1)
                dve.wait_ge(adj_loaded, 32)
                dve.tensor_scalar(mask[:], adj[:], 0.0, MASKED, ALU.is_equal, ALU.mult).then_inc(dve_setup, 1)
                dve.wait_ge(wqkv_loaded, 16)
                dve.tensor_copy(wqk_hi[:], wqkv[:, 0:2 * D]).then_inc(qk_split, 1)
                dve.wait_ge(qk_split, 1)
                dve.tensor_tensor(wqk_lo[:], wqkv[:, 0:2 * D], wqk_hi[:].bitcast(F32), ALU.subtract) \
                   .then_inc(qk_split, 1)
                dve.wait_ge(pool_setup, 9)
                dve.tensor_tensor(anorm[:], adj[:], ident[:], ALU.add).then_inc(dve_setup, 1)
                dve.tensor_tensor(anorm_t[:], adjt[:], ident[:], ALU.add).then_inc(dve_setup, 1)
                dve.tensor_reduce(degs[:, 2:3], adj_split_t[:, 0, :], AX_X, ALU.add).then_inc(dve_setup, 1)
                dve.wait_ge(dve_setup, 4)
                dve.tensor_reduce(degs[:, 0:1], anorm[:], AX_X, ALU.add).then_inc(dve_setup, 1)
                dve.tensor_reduce(degs[:, 1:2], anorm_t[:], AX_X, ALU.add).then_inc(dve_setup, 1)
                dve.wait_ge(dve_setup, 6)
                dve.tensor_tensor(degs[:, 3:4], degs[:, 0:1], degs[:, 1:2], ALU.add).then_inc(dve_setup, 1)
                dve.wait_ge(dve_setup, 7)
                dve.scalar_tensor_tensor(degs[:, 4:5], degs[:, 3:4], -1.0, degs[:, 2:3],
                                         ALU.add, ALU.subtract).then_inc(dve_setup, 1)
                dve.wait_ge(pool_setup, 10)
                dve.tensor_scalar(anorm[:], anorm[:], degs[:, 5:6], None, ALU.mult).then_inc(dve_setup, 1)
                dve.wait_ge(pe_setup, 1)
                dve.tensor_scalar(ahat_t[:], bank[0][:, 0:N], degs[:, 5:6], None, ALU.mult).then_inc(dve_setup, 1)
                dve.wait_ge(pe_setup, 2)
                dve.tensor_copy(row_bias[:], bank[1][:, 0:3 * D].rearrange("p (a d) -> p a d", a=3)) \
                   .then_inc(dve_setup, 1)

            @block.tensor
            def _(pe):
                pe.wait_ge(dve_setup, 9)
                pe.wait_ge(pool_setup, 6)
                pe.transpose(bank[0][:, 0:N], anorm[:], ident[:]).then_inc(pe_setup, 1)
                pe.wait_ge(rows_loaded, 16)
                pe.matmul(bank[1][:, 0:3 * D], ones_row[:], rows[:].rearrange("p a d -> p (a d)"),
                          start=True, stop=True).then_inc(pe_setup, 1)

        X, P, A, L, Y, H, S = -2, -1, 0, 1, 2, 3, 4

        q_mm, k_mm, v_mm = sem("q_mm"), sem("k_mm"), sem("v_mm")
        q_out, k_out, v_out = sem("q_out"), sem("k_out"), sem("v_out")
        score_mm, score_max, exp_done = sem("score_mm"), sem("score_max"), sem("exp_done")
        pt_mm, pt_out = sem("pt_mm"), sem("pt_out")
        av_mm, av_recip, av_out = sem("av_mm"), sem("av_recip"), sem("av_out")
        s0_done, st0, mv0, ve0, rs0, x1_done, x1b_done = (
            sem("s0_done"), sem("st0"), sem("mv0"), sem("ve0"), sem("rs0"), sem("x1_done"), sem("x1b_done"))
        y_mm, y_out, z_mm = sem("y_mm"), sem("y_out"), sem("z_mm")
        s1_done, st1, mv1, ve1, rs1, x2_done, x2_kept = (
            sem("s1_done"), sem("st1"), sem("mv1"), sem("ve1"), sem("rs1"), sem("x2_done"), sem("x2_kept"))
        g_hi = sem("g_hi")
        g_mm, g_out, h_mm, h_out, h_stat = sem("g_mm"), sem("g_out"), sem("h_mm"), sem("h_out"), sem("h_stat")

        R0, R1, S0, S1, PTB, OB, YB, ZB = bank

        with nc.Block() as block:
            @block.sync
            def _(sp):
                def load_xt(par, group):
                    sp.dma_start(xt_in[:, par, :], io["xt"][:, ds(group * T, T)]).then_inc(xt_ld[par], 16)

                def load_xg(par, group):
                    sp.dma_start(xg[:, par, :], io["x"][:, ds(group * T, T)]).then_inc(xg_ld[par], 16)

                def turn(t):
                    if t.has(P):
                        sp.wait_ge(bufs_set, 3)
                        need(sp, q_out, t.group(P) + 1)
                        need(sp, score_mm, (t.group(P) - 1) * GB)
                        for h in range(HEADS):
                            sp.dma_start(q_head[HD * h:HD * (h + 1), t.par(P), h, :],
                                         q_all[HD * h:HD * (h + 1), :]).then_inc(qh_ld[t.par(P)], 16)
                        if not t.peeled or t.c - P + 2 < G:
                            need(sp, v_mm, t.group(P) + 1)
                            load_xt(t.par(P), t.group(P) + 2)
                    if t.has(L) and (not t.peeled or t.c - L + 2 < G):
                        need(sp, s0_done, t.group(L) + 1)
                        load_xg(t.par(L), t.group(L) + 2)

                turns(sp, turn, -1, 3, G - 3, G + 1)

            @block.tensor
            def _(pe):
                pe.wait_ge(wqkv_loaded, 16)
                pe.wait_ge(qk_split, 2)

                def split_product(out, weights, data):
                    for k, (w, x) in enumerate(((0, 0), (1, 0), (0, 1))):
                        mm = pe.matmul(out, weights[w], data[x], start=(k == 0), stop=(k == 2))
                    return mm

                def aggregate(t, j):
                    if t.peeled and t.c == Y and j == 0:
                        pe.wait_ge(late_split, 4)
                    if j % 2 == 0:
                        need(pe, x1_lo_done, t.group(Y) * 2 + (j // 2 + 1))
                    need(pe, y_out, t.group(Y) * GB + j)
                    split_product(YB[:, 0:3 * N],
                                  [part[:, t.par(Y), j * D:(j + 1) * D] for part in (x1_hi, x1_lo)],
                                  (adj3_hi[:], adj3_lo[:])).then_inc(y_mm, 1)

                def turn(t):
                    for j in range(GB):
                        s = t.group(A) * GB + j
                        if t.has(A):
                            if j == 0:
                                need(pe, qh_ld[t.par(A)], (t.half(A) + 1) * 16 * HEADS)
                                need(pe, k_out, t.group(A) + 1)
                            need(pe, score_max, s - 1)
                            out = (S0, S1)[j % 2]
                            for h in range(HEADS):
                                mm = pe.matmul(out[:, h * N:(h + 1) * N], q_head[:, t.par(A), h, j * N:(j + 1) * N],
                                               k_t[:, t.par(A), j * N:(j + 1) * N], start=True, stop=True)
                            mm.then_inc(score_mm, 1)
                        if t.has(Y) and j >= 1:
                            aggregate(t, j)
                        lag = A if j >= 1 else L
                        if t.has(lag):
                            need(pe, exp_done, s)
                            need(pe, pt_out, s - 1)
                            for h in range(HEADS):
                                mm = pe.transpose(PTB[:, h * N:(h + 1) * N],
                                                  probs[:, (j + 1) % 2, h * N:(h + 1) * N], ident[:])
                            mm.then_inc(pt_mm, 1)
                        if t.has(Y) and j == 0:
                            aggregate(t, j)
                        if t.has(P):
                            par = t.par(P)
                            if j == 0:
                                need(pe, xt_lo_done, t.group(P) + 1)
                                need(pe, v_out, t.group(P))
                                need(pe, h_out, (t.group(P) - 4) * HID)
                                split_product(R0[:], (wqk_hi[:, 0:D], wqk_lo[:, 0:D]),
                                              (xt_hi[:, par, :], xt_lo[:, par, :])).then_inc(q_mm, 1)
                            if j == 1:
                                need(pe, k_out, t.group(P))
                                need(pe, h_out, (t.group(P) - 4) * HID)
                                split_product(R1[:], (wqk_hi[:, D:2 * D], wqk_lo[:, D:2 * D]),
                                              (xt_hi[:, par, :], xt_lo[:, par, :])).then_inc(k_mm, 1)
                            if j == 2:
                                need(pe, q_out, t.group(P) + 1)
                                for b in range(GB):
                                    mm = pe.matmul(R0[:, b * D:(b + 1) * D], xt_in[:, par, b * N:(b + 1) * N],
                                                   wqkv[:, 2 * D:3 * D], start=True, stop=True)
                                mm.then_inc(v_mm, 1)
                        lag = A if j >= 2 else L
                        if t.has(lag):
                            vb = (j - 2) % GB
                            need(pe, pt_out, s - 1)
                            need(pe, av_out, s - 2)
                            need(pe, v_out, t.group(lag) + 1)
                            for h in range(HEADS):
                                mm = pe.matmul(OB[:, h * VW:(h + 1) * VW], probs_t[:, j % 2, h * N:(h + 1) * N],
                                               v_one[:, t.par(lag), vb, h * VW:(h + 1) * VW], start=True, stop=True)
                            mm.then_inc(av_mm, 1)
                        if t.has(H) and j == 2:
                            need(pe, x2_done, t.group(H) + 1)
                            need(pe, h_out, t.group(H) * HID)
                            if t.has(P):
                                need(pe, k_out, t.group(P) + 1)
                            for b in range(GB):
                                mm = pe.matmul(R1[:, b * N:(b + 1) * N], x2[:, b * D:(b + 1) * D],
                                               ahat_t[:], start=True, stop=True)
                            mm.then_inc(g_mm, 1)
                        if t.has(Y):
                            if t.peeled and t.c == Y and j == 0:
                                pe.wait_ge(w_l1_loaded, 16)
                            need(pe, y_out, t.group(Y) * GB + j + 1)
                            if j == 0:
                                need(pe, s1_done, t.group(Y))
                            for k in range(3):
                                mm = pe.matmul(ZB[:, j * D:(j + 1) * D], agg3[:, j % 2, k * N:(k + 1) * N],
                                               w_l1[:, k, :], start=(k == 0), stop=(k == 2))
                            mm.then_inc(z_mm, 1)
                        if t.has(H) and j == 3:
                            need(pe, g_lo, t.group(H) + 1)
                            need(pe, h_out, t.group(H) * HID)
                            if t.has(P):
                                need(pe, v_out, t.group(P) + 1)
                            for k, out in enumerate((R0, R1)):
                                cols = slice(k * 128, (k + 1) * 128)
                                split_product(out[:], (w1t_hi[:, cols], w1t_lo[:, cols]),
                                              (agg_hi[:], agg_lo[:])).then_inc(h_mm, 1)

                turns(pe, turn, -1, 4, G - 2, G + 3)

            @block.scalar
            def _(act):
                def turn(t):
                    for j in range(GB):
                        s = t.group(A) * GB + j
                        if t.has(Y):
                            y = t.group(Y) * GB + j
                            need(act, y_mm, y + 1)
                            need(act, z_mm, y - 1)
                            act.copy(agg3[:, j % 2, :], YB[:, 0:3 * N]).then_inc(y_out, 1)
                        if t.has(X) and j == 0:
                            need(act, xt_ld[t.par(X)], (t.half(X) + 1) * 16)
                            need(act, k_mm, t.group(X) - 1)
                            act.copy(xt_hi[:, t.par(X), :], xt_in[:, t.par(X), :]).then_inc(xt_hi_done, 1)
                        if t.has(P) and j == 0:
                            need(act, q_mm, t.group(P) + 1)
                            need(act, qh_ld[1 - t.par(P)], t.half(P + 1) * 16 * HEADS + 16 * HEADS)
                            act.mul(q_all, R0[:], HD ** -0.5).then_inc(q_out, 1)
                        if t.has(A):
                            need(act, score_max, s + 1)
                            need(act, pt_mm, s - 1)
                            for h in range(HEADS):
                                e = act.activation(probs[:, j % 2, h * N:(h + 1) * N],
                                                   scores[:, j % 2, h * N:(h + 1) * N], ACT.Exp,
                                                   bias=neg_max[:, j % 2, h:h + 1], scale=-1.0)
                            e.then_inc(exp_done, 1)
                        if t.has(H) and j == 2:
                            need(act, g_mm, t.group(H) + 1)
                            need(act, h_mm, t.group(H) * HID)
                            act.copy(agg_hi[:], R1[:]).then_inc(g_hi, 1)
                            act.copy(agg_t, R1[:]).then_inc(g_out, 1)
                        if t.has(L) and j == 3:
                            need(act, x1_done, t.group(L) + 1)
                            need(act, y_mm, (t.group(L) - 1) * GB)
                            for half in range(2):
                                cols = slice(half * (T // 2), (half + 1) * (T // 2))
                                act.copy(x1_hi[:, t.par(L), cols], x1[:, t.par(L), cols]).then_inc(x1_hi_done, 1)
                        if t.has(H) and j == 3:
                            for k, src in enumerate((R0, R1)):
                                need(act, h_mm, t.group(H) * HID + k + 1)
                                act.activation(wide[k][:, ds(t.group(H) * T, T)], src[:], ACT.Identity,
                                               bias=bn1p[:, 0, k:k + 1]).then_inc(h_out, 1)

                turns(act, turn, -2, 4, G - 2, G + 3)

            @block.vector
            def _(dve):
                def carry_waits(word):
                    dve.memset(idle_words[:, word:word + 1], 0.0)

                def ln_stats(i, src, stat_sem, mv_sem, group):
                    for b in range(GB):
                        dve.bn_stats(ln_st[:, i, b, :], src[:, b * D:(b + 1) * D]).then_inc(stat_sem, 1)
                    need(dve, stat_sem, (group + 1) * GB)
                    carry_waits(GB + i)
                    for b in range(GB):
                        dve.bn_aggr(ln_mv[:, i, b, :], ln_st[:, i, b, :]).then_inc(mv_sem, 1)

                def ln_apply(i, src, dst, done):
                    for b in range(GB):
                        op = dve.tensor_scalar(dst[:, b * D:(b + 1) * D], src[:, b * D:(b + 1) * D],
                                               ln_mv[:, i, b, 0:1], ln_rs[:, i, b:b + 1], ALU.subtract, ALU.mult)
                    op.then_inc(done, 1)

                def turn(t):
                    for j in range(GB):
                        s = t.group(A) * GB + j
                        if t.has(H) and j == 0:
                            need(dve, z_mm, (t.group(H) + 1) * GB)
                            need(dve, x1b_done, t.group(H) + 1)
                            dve.tensor_tensor(s1, ZB[:], x1[:, t.par(H), :], ALU.add).then_inc(s1_done, 1)
                        if t.has(A):
                            need(dve, score_mm, s + 1)
                            need(dve, exp_done, s - 1)
                            carry_waits(j)
                            for h in range(HEADS):
                                cols = slice(h * N, (h + 1) * N)
                                op = dve.tensor_tensor_reduce(scores[:, j % 2, cols], (S0, S1)[j % 2][:, cols], mask[:],
                                                              -1.0, 3.0e38, ALU.add, ALU.min,
                                                              neg_max[:, j % 2, h:h + 1])
                            op.then_inc(score_max, 1)
                        if t.has(A if j >= 1 else L):
                            need(dve, pt_mm, s)
                            need(dve, av_mm, s - 2)
                            dve.tensor_copy(probs_t[:, (j + 1) % 2, :], PTB[:]).then_inc(pt_out, 1)
                        if t.has(P) and j == 1:
                            need(dve, k_mm, t.group(P) + 1)
                            need(dve, score_mm, (t.group(P) - 1) * GB)
                            dve.tensor_copy(k_t[:, t.par(P), :], R1[:]).then_inc(k_out, 1)
                        if t.has(P) and j == 2:
                            need(dve, v_mm, t.group(P) + 1)
                            need(dve, av_mm, (t.group(P) - 1) * GB)
                            dve.tensor_copy(
                                v_one[:, t.par(P), :, :].rearrange("p b (h v) -> p (b h) v", v=VW)[:, :, 0:HD],
                                R0[:].rearrange("p (c v) -> p c v", v=HD)).then_inc(v_out, 1)
                        lag = A if j >= 2 else L
                        if t.has(lag):
                            o = OB[:, 0:HEADS * VW].rearrange("p (h v) -> p h v", v=VW)
                            need(dve, av_mm, s - 1)
                            dve.reciprocal(recip, o[:, :, HD]).then_inc(av_recip, 1)
                            need(dve, av_recip, s - 1)
                            b = (j - 2) % GB
                            dve.tensor_tensor(
                                attn[:, t.par(lag), b * D:(b + 1) * D].rearrange("p (h v) -> p h v", v=HD),
                                o[:, :, 0:HD], recip.unsqueeze(2).broadcast_to([N, HEADS, HD]),
                                ALU.mult).then_inc(av_out, 1)
                        if t.has(H) and j == 0:
                            need(dve, s1_done, t.group(H) + 1)
                            need(dve, ve1, t.group(H))
                            ln_stats(1, s1, st1, mv1, t.group(H))
                        if t.has(S) and j == 0:
                            for k in range(HID):
                                need(dve, h_out, t.group(S) * HID + k + 1)
                                dve.bn_stats(bn_stats1[:, k, ds(t.group(S), 1), :].rearrange("p a s -> p (a s)"),
                                             wide[k][:, ds(t.group(S) * T, T)]).then_inc(h_stat, 1)
                        if t.has(H) and j == 1:
                            need(dve, rs1, t.group(H) + 1)
                            need(dve, g_mm, t.group(H))
                            need(dve, x2_kept, t.group(H))
                            ln_apply(1, s1, x2, x2_done)
                        if t.has(L) and j == 2:
                            need(dve, s0_done, t.group(L) + 1)
                            ln_stats(0, attn[:, t.par(L), :], st0, mv0, t.group(L))
                        if t.has(L) and j == 3:
                            need(dve, rs0, t.group(L) + 1)
                            need(dve, x1b_done, t.group(L) - 1)
                            ln_apply(0, attn[:, t.par(L), :], x1[:, t.par(L), :], x1_done)

                turns(dve, turn, -1, 6, G - 2, G + 4)

            @block.gpsimd
            def _(pool):
                def rstd(i, mv_sem, eps_sem, done, group):
                    need(pool, mv_sem, (group + 1) * GB)
                    pool.tensor_tensor(ln_rs[:, i, :], ln_mv[:, i, :, 1], eps_tile, ALU.add).then_inc(eps_sem, 1)
                    need(pool, eps_sem, group + 1)
                    pool.tensor_tensor(ln_rs[:, i, :], ln_rs[:, i, :], neg_half, ALU.pow).then_inc(done, 1)

                def turn(t):
                    if t.has(X):
                        need(pool, xt_hi_done, t.group(X) + 1)
                        pool.tensor_tensor(xt_lo[:, t.par(X), :], xt_in[:, t.par(X), :],
                                           xt_hi[:, t.par(X), :].bitcast(F32), ALU.subtract).then_inc(xt_lo_done, 1)
                    if t.peeled and t.c == -1:
                        pool.wait_ge(mlp1_loaded, 32)
                        adj3 = adj_split_t[:].rearrange("p a n -> p (a n)")
                        pool.tensor_copy(adj3_hi[:], adj3).then_inc(late_split, 1)
                        pool.tensor_copy(w1t_hi[:], w1t[:]).then_inc(late_split, 1)
                        pool.wait_ge(late_split, 2)
                        pool.tensor_tensor(adj3_lo[:], adj3, adj3_hi[:].bitcast(F32), ALU.subtract) \
                            .then_inc(late_split, 1)
                        pool.tensor_tensor(w1t_lo[:], w1t[:], w1t_hi[:].bitcast(F32), ALU.subtract) \
                            .then_inc(late_split, 1)
                    if t.has(H):
                        need(pool, x2_done, t.group(H))
                        rstd(1, mv1, ve1, rs1, t.group(H))
                    if t.has(L):
                        need(pool, av_out, (t.group(L) + 1) * GB)
                        need(pool, xg_ld[t.par(L)], (t.half(L) + 1) * 16)
                        pool.tensor_tensor(attn[:, t.par(L), :], attn[:, t.par(L), :], xg[:, t.par(L), :], ALU.add).then_inc(s0_done, 1)
                    if t.has(H):
                        need(pool, x2_done, t.group(H) + 1)
                        pool.tensor_copy(xres[:, ds(t.group(H) * GB, GB), :].rearrange("p b d -> p (b d)"),
                                         x2).then_inc(x2_kept, 1)
                    if t.has(L):
                        rstd(0, mv0, ve0, rs0, t.group(L))
                    if t.has(H):
                        need(pool, g_out, t.group(H) + 1)
                        pool.tensor_tensor(agg_lo[:], agg_t, agg_hi[:].bitcast(F32), ALU.subtract).then_inc(g_lo, 1)
                    if t.has(L):
                        for half in range(2):
                            cols = slice(half * (T // 2), (half + 1) * (T // 2))
                            need(pool, x1_hi_done, t.group(L) * 2 + (half + 1))
                            pool.tensor_tensor(x1_lo[:, t.par(L), cols], x1[:, t.par(L), cols],
                                               x1_hi[:, t.par(L), cols].bitcast(F32), ALU.subtract) \
                                .then_inc(x1_lo_done, 1)
                        need(pool, x1_lo_done, t.group(L) * 2 + 2)
                        pool.tensor_tensor(x1[:, t.par(L), :].rearrange("p (b d) -> p b d", d=D),
                                           x1[:, t.par(L), :].rearrange("p (b d) -> p b d", d=D),
                                           row_bias[:, 0:1, :].broadcast_to([N, GB, D]),
                                           ALU.add).then_inc(x1b_done, 1)

                turns(pool, turn, -2, 4, G - 2, G + 3)

        work_a.close()
        wih_hi, wih_lo, whh_hi, whh_lo = (
            sb(n, [D, STEPS, GATES * D], F32R) for n in ("wih_hi", "wih_lo", "whh_hi", "whh_lo"))
        work_b = ctx.enter_context(ExitStack())
        work = sb("work_b", [128, WORK_B], side="right", scope=work_b)
        spot[0] = 0
        hid = carve(2, HID, T)
        stage = sb("stage", [D, 2 * STEPS * GATES * D], side="right", scope=work_b)
        stage_loaded = sem("stage_loaded")
        bn_eps, bn_rstd, bn_dve, w_split = sem("bn_eps"), sem("bn_rstd"), sem("bn_dve"), sem("w_split")
        bias_sum = sem("bias_sum")
        relu_done, mlp_mm, y2_out, y2_stat = sem("relu_done"), sem("mlp_mm"), sem("y2_out"), sem("y2_stat")

        def bn_finish_dve(dve, slots, stats, gain, offset, before):
            f = bn_fin[:, slots, :]
            for k, st in enumerate(stats):
                dve.bn_aggr(f[:, k, 0:2], st).then_inc(bn_dve, 1)
            before += len(stats)
            dve.wait_ge(bn_rstd, 1 if slots.start == 0 else 2)
            dve.tensor_tensor(f[:, :, 4], f[:, :, 3], gain, ALU.mult).then_inc(bn_dve, 1)
            dve.wait_ge(bn_dve, before + 1)
            dve.tensor_tensor(bn_tmp[:, slots], f[:, :, 0], f[:, :, 4], ALU.mult).then_inc(bn_dve, 1)
            dve.wait_ge(bn_dve, before + 2)
            dve.tensor_tensor(f[:, :, 5], offset, bn_tmp[:, slots], ALU.subtract).then_inc(bn_dve, 1)

        def bn_finish_pool(pool, slots, blocks, before):
            f = bn_fin[:, slots, :]
            n = 1 if slots.start == 0 else 2
            pool.wait_ge(bn_dve, before + blocks)
            pool.tensor_tensor(f[:, :, 2], f[:, :, 1], eps_tile[:, 0:blocks], ALU.add).then_inc(bn_eps, 1)
            pool.wait_ge(bn_eps, n)
            pool.tensor_tensor(f[:, :, 3], f[:, :, 2], neg_half[:, 0:blocks], ALU.pow).then_inc(bn_rstd, 1)

        MLP1, MLP2 = slice(0, HID), slice(HID, HID + 1)
        BN1_OPS = HID + 3

        with nc.Block() as block:
            @block.vector
            def _(dve):
                bn_finish_dve(dve, MLP1, [bn_stats1[:, k, :, :].rearrange("p g s -> p (g s)") for k in range(HID)],
                              bn1p[:, 1, :], bn1p[:, 2, :], 0)
                dve.wait_ge(rest_loaded, 16 * REST_LOADS)
                dve.tensor_tensor(gate_bias[:], lstm_b[:, 0, :], lstm_b[:, 1, :], ALU.add).then_inc(bias_sum, 1)

                def turn(t):
                    g = t.group(0)
                    cols = ds(g * T, T)
                    need(dve, mlp_mm, g + 1)
                    dve.tensor_scalar(wide0[:, cols], bank[t.par(0)][:], bn2p[:, 0:1], None, ALU.add) \
                       .then_inc(y2_out, 1)
                    need(dve, y2_out, g + 1)
                    dve.bn_stats(bn_stats2[:, ds(g, 1), :].rearrange("p a s -> p (a s)"), wide0[:, cols]) \
                       .then_inc(y2_stat, 1)

                turns(dve, turn, 0, 2, G, G)

            @block.sync
            def _(sp):
                sp.dma_start(stage[:], io["lstm_w"]).then_inc(stage_loaded, 16)

            @block.gpsimd
            def _(pool):
                bn_finish_pool(pool, MLP1, HID, 0)
                pool.wait_ge(stage_loaded, 16)
                for n, (hi, lo) in enumerate(((wih_hi, wih_lo), (whh_hi, whh_lo))):
                    raw = stage[:, n * STEPS * GATES * D:(n + 1) * STEPS * GATES * D]
                    pool.tensor_copy(hi[:].rearrange("k s g -> k (s g)"), raw).then_inc(w_split, 1)
                    pool.wait_ge(w_split, 2 * n + 1)
                    pool.tensor_tensor(lo[:].rearrange("k s g -> k (s g)"), raw,
                                       hi[:].rearrange("k s g -> k (s g)").bitcast(F32),
                                       ALU.subtract).then_inc(w_split, 1)

            @block.scalar
            def _(act):
                act.wait_ge(bn_dve, BN1_OPS)

                def turn(t):
                    g = t.group(0)
                    need(act, mlp_mm, g - 1)
                    for k in range(HID):
                        act.activation(hid[:, t.par(0), k, :], wide[k][:, ds(g * T, T)], ACT.Relu,
                                       bias=bn_fin[:, k, 5:6], scale=bn_fin[:, k, 4:5]).then_inc(relu_done, 1)

                turns(act, turn, 0, 2, G, G)

            @block.tensor
            def _(pe):
                pe.wait_ge(rest_loaded, 16 * REST_LOADS)

                def turn(t):
                    g = t.group(0)
                    need(pe, y2_out, g - 1)
                    for k in range(HID):
                        need(pe, relu_done, g * HID + k + 1)
                        mm = pe.matmul(bank[t.par(0)][:], w2t[:, k, :], hid[:, t.par(0), k, :],
                                       start=(k == 0), stop=(k == HID - 1))
                    mm.then_inc(mlp_mm, 1)

                turns(pe, turn, 0, 2, G, G)

        work_b.close()
        early.close()
        st_hi, st_lo = sb("st_hi", [D, TOKENS], F32R), sb("st_lo", [D, TOKENS], F32R)
        work_c = ctx.enter_context(ExitStack())
        work = sb("work_c", [128, WORK_C], side="right", scope=work_c)
        spot[0] = 0
        y_bn = carve(2, T)
        s2 = carve(2, T)
        x3 = carve(2, T)
        x3_t = carve(T)
        u0 = carve(T)
        v0 = carve(T)
        u1 = carve(T)
        v1 = carve(T)
        ln2_st = carve(2, GB, 6)
        ln2_mv = carve(2, GB, 2)
        ln2_ve = carve(2, GB)
        ln2_rs = carve(2, GB)
        ln2_sh = carve(2, GB)
        BT, XT, U0, V0, U1, V1 = bank[0:6]
        ybn_done, bt_mm, s2_done, st2, mv2, ve2, rs2 = (
            sem("ybn_done"), sem("bt_mm"), sem("s2_done"), sem("st2"), sem("mv2"), sem("ve2"), sem("rs2"))
        rm2, sh2, x3_dve, x3_act = sem("rm2"), sem("sh2"), sem("x3_dve"), sem("x3_act")
        x3_kept = [sem(f"x3_kept{i}") for i in range(2)]
        xt_mm, xt_out = sem("xt_mm"), sem("xt_out")
        u0_mm, u0_out, v0_mm, v0_out = sem("u0_mm"), sem("u0_out"), sem("v0_mm"), sem("v0_out")
        u1_mm, u1_out, v1_mm, v1_out = sem("u1_mm"), sem("u1_out"), sem("v1_mm"), sem("v1_out")
        v1_hi, v1_lo = sem("v1_hi"), sem("v1_lo")

        def by_batch(a):
            return a.rearrange("p (b d) -> p b d", d=D)

        with nc.Block() as block:
            @block.tensor
            def _(pe):
                def four(out, lhs, rhs, done):
                    for b in range(GB):
                        cols = slice(b * 128, (b + 1) * 128)
                        if rhs is None:
                            mm = pe.transpose(out[:, cols], lhs[:, cols], ident[:])
                        else:
                            mm = pe.matmul(out[:, cols], lhs[:, cols], rhs, start=True, stop=True)
                    mm.then_inc(done, 1)

                def turn(t):
                    if t.has(3):
                        need(pe, xt_out, t.group(3) + 1)
                        need(pe, u0_out, t.group(3))
                        four(U0, x3_t, wg[:, 0, :], u0_mm)
                    if t.has(0):
                        need(pe, ybn_done, t.group(0) + 1)
                        need(pe, s2_done, t.group(0))
                        four(BT, y_bn[:, t.par(0), :], None, bt_mm)
                    if t.has(4):
                        need(pe, v0_out, t.group(4) + 1)
                        need(pe, u1_out, t.group(4))
                        four(U1, v0, wg[:, 1, :], u1_mm)
                    if t.has(2):
                        need(pe, x3_dve, t.group(2) + 1)
                        need(pe, x3_act, t.group(2) + 1)
                        need(pe, xt_out, t.group(2))
                        four(XT, x3[:, t.par(2), :], None, xt_mm)
                    if t.has(3):
                        need(pe, u0_out, t.group(3) + 1)
                        need(pe, v0_out, t.group(3))
                        four(V0, u0, adjt[:], v0_mm)
                    if t.has(4):
                        need(pe, u1_out, t.group(4) + 1)
                        need(pe, v1_out, t.group(4))
                        four(V1, u1, adjt[:], v1_mm)

                turns(pe, turn, 0, 6, G, G + 4)

            def x3_free(eng, t):
                need(eng, xt_mm, t.group(1) - 1)
                if not t.peeled or t.c - 1 >= 2:
                    need(eng, x3_kept[t.par(1)], t.half(1) * 16)

            ON_ACT = 2

            @block.scalar
            def _(act):
                act.wait_ge(bn_dve, BN1_OPS + 4)

                def turn(t):
                    if t.has(5):
                        need(act, v1_mm, t.group(5) + 1)
                        act.activation(st_hi[:, ds(t.group(5) * T, T)], V1[:], ACT.Relu).then_inc(v1_hi, 1)
                        need(act, v1_lo, t.group(5))
                        act.activation(v1, V1[:], ACT.Relu).then_inc(v1_out, 1)
                    if t.has(-1):
                        need(act, bt_mm, t.group(-1) - 1)
                        act.activation(y_bn[:, t.par(-1), :], wide0[:, ds(t.group(-1) * T, T)], ACT.Identity,
                                       bias=bn_fin[:, HID, 5:6], scale=bn_fin[:, HID, 4:5]).then_inc(ybn_done, 1)
                    if t.has(1):
                        need(act, sh2, t.group(1) + 1)
                        x3_free(act, t)
                        p = t.par(1)
                        for b in range(GB - ON_ACT, GB):
                            op = act.activation(x3[:, p, b * D:(b + 1) * D], s2[:, p, b * D:(b + 1) * D],
                                                ACT.Identity, bias=ln2_sh[:, p, b:b + 1], scale=ln2_rs[:, p, b:b + 1])
                        op.then_inc(x3_act, 1)
                    if t.has(2):
                        need(act, xt_mm, t.group(2) + 1)
                        need(act, u0_mm, t.group(2))
                        act.copy(x3_t, XT[:]).then_inc(xt_out, 1)
                    if t.has(3):
                        need(act, v0_mm, t.group(3) + 1)
                        need(act, u1_mm, t.group(3))
                        act.activation(v0, V0[:], ACT.Relu).then_inc(v0_out, 1)

                turns(act, turn, -1, 7, G - 1, G + 5)

            @block.vector
            def _(dve):
                bn_finish_dve(dve, MLP2, [bn_stats2[:].rearrange("p g s -> p (g s)")], bn2p[:, 1:2], bn2p[:, 2:3],
                              BN1_OPS)

                def turn(t):
                    p = t.par(0)
                    if t.has(3):
                        need(dve, u0_mm, t.group(3) + 1)
                        need(dve, v0_mm, t.group(3))
                        dve.tensor_tensor(by_batch(u0), by_batch(U0[:]), row_bias[:, 1:2, :].broadcast_to([N, GB, D]),
                                          ALU.add).then_inc(u0_out, 1)
                    if t.has(0):
                        g = t.group(0)
                        need(dve, bt_mm, g + 1)
                        need(dve, x3_act, g - 1)
                        dve.tensor_tensor(by_batch(s2[:, p, :]), by_batch(BT[:]), xres[:, ds(g * GB, GB), :],
                                          ALU.add).then_inc(s2_done, 1)
                    if t.has(4):
                        need(dve, u1_mm, t.group(4) + 1)
                        need(dve, v1_mm, t.group(4))
                        dve.tensor_tensor(by_batch(u1), by_batch(U1[:]), row_bias[:, 2:3, :].broadcast_to([N, GB, D]),
                                          ALU.add).then_inc(u1_out, 1)
                    if t.has(1):
                        q = t.par(1)
                        need(dve, rs2, t.group(1) + 1)
                        x3_free(dve, t)
                        for b in range(GB - ON_ACT):
                            op = dve.tensor_scalar(x3[:, q, b * D:(b + 1) * D], s2[:, q, b * D:(b + 1) * D],
                                                   ln2_mv[:, q, b, 0:1], ln2_rs[:, q, b:b + 1], ALU.subtract, ALU.mult)
                        op.then_inc(x3_dve, 1)
                    if t.has(0):
                        need(dve, s2_done, t.group(0) + 1)
                        for b in range(GB):
                            dve.bn_stats(ln2_st[:, p, b, :], s2[:, p, b * D:(b + 1) * D]).then_inc(st2, 1)
                        need(dve, st2, (t.group(0) + 1) * GB)
                        need(dve, sh2, t.group(0) - 1)
                        dve.memset(idle_words[:, p:p + 1], 0.0)
                        for b in range(GB):
                            dve.bn_aggr(ln2_mv[:, p, b, :], ln2_st[:, p, b, :]).then_inc(mv2, 1)

                turns(dve, turn, 0, 6, G, G + 4)

            @block.gpsimd
            def _(pool):
                bn_finish_pool(pool, MLP2, 1, BN1_OPS)

                def turn(t):
                    if t.has(5):
                        cols = ds(t.group(5) * T, T)
                        need(pool, v1_out, t.group(5) + 1)
                        pool.tensor_tensor(st_lo[:, cols], v1, st_hi[:, cols].bitcast(F32), ALU.subtract) \
                            .then_inc(v1_lo, 1)
                    if t.has(0):
                        g, p = t.group(0), t.par(0)
                        need(pool, mv2, (g + 1) * GB)
                        pool.tensor_tensor(ln2_ve[:, p, :], ln2_mv[:, p, :, 1], eps_tile, ALU.add).then_inc(ve2, 1)
                        need(pool, ve2, g + 1)
                        need(pool, x3_dve, g - 1)
                        need(pool, x3_act, g - 1)
                        pool.tensor_tensor(ln2_rs[:, p, :], ln2_ve[:, p, :], neg_half, ALU.pow).then_inc(rs2, 1)
                        need(pool, rs2, g + 1)
                        pool.tensor_tensor(ln2_sh[:, p, :], ln2_mv[:, p, :, 0], ln2_rs[:, p, :], ALU.mult) \
                            .then_inc(rm2, 1)
                        need(pool, rm2, g + 1)
                        pool.tensor_tensor(ln2_sh[:, p, :], zero_wide[:, 0:GB], ln2_sh[:, p, :], ALU.subtract) \
                            .then_inc(sh2, 1)
                turns(pool, turn, 0, 6, G, G + 5)

            @block.sync
            def _(sp):
                def turn(t):
                    g = t.group(0)
                    need(sp, x3_dve, g + 1)
                    need(sp, x3_act, g + 1)
                    sp.dma_start(xres[:, ds(g * GB, GB), :], by_batch(x3[:, t.par(0), :])) \
                        .then_inc(x3_kept[t.par(0)], 16)

                turns(sp, turn, 0, 2, G, G)
                for par in range(2):
                    sp.wait_ge(x3_kept[par], 16 * (G // 2))

        work_c.close()
        hidden.close()
        C = 512
        I_, F_, G_, O_ = range(GATES)

        def tiles(name, shape, dt=F32):
            return [sb(f"{name}{a}", shape, dt, side="right") for a in range(2)]

        mid_hi, mid_lo = tiles("mid_hi", [D, C], F32R), tiles("mid_lo", [D, C], F32R)
        act_i, act_f, act_g, act_o, cell, fc, h_new = (
            tiles(n, [D, C]) for n in ("act_i", "act_f", "act_g", "act_o", "cell", "fc", "h_new"))

        def pair(name):
            return [sem(f"{name}{a}") for a in range(2)]

        gate_mm, gate_out, cell_ops, cell_done, tanh_done, h_full, h_hi, h_lo = map(pair, (
            "gate_mm", "gate_out", "cell_ops", "cell_done", "tanh_done", "h_full", "h_hi", "h_lo"))

        class Pass:
            pass

        passes = []
        steps_before = gates_before = mids_before = 0
        for p, (nb, nw) in {1: (GB, N), 2: (8, 64), 3: (32, 14), 4: (16, 32)}.items():
            ps = Pass()
            ps.p, ps.nb, ps.nw, ps.cols = p, nb, nw, nb * nw
            ps.across = (N // p) // nw
            ps.rounds = (B // nb) * ps.across // 2
            ps.steps_before, ps.gates_before, ps.mids_before = steps_before, gates_before, mids_before
            ps.gates = 3 + GATES * (p - 1)
            steps_before += ps.rounds * p
            gates_before += ps.rounds * ps.gates
            mids_before += ps.rounds * (p - 1)
            assert ps.across * nw == N // p and ps.cols <= C
            passes.append(ps)

        class Step:

            def __init__(self, ps, i, t):
                self.ps, self.t, self.first, self.last = ps, t, t == 0, t == ps.p - 1
                self.gates = (I_, G_, O_) if self.first else (F_, I_, G_, O_)
                self.n = i * ps.p + (ps.steps_before + t)
                self.gates_before = i * ps.gates + (ps.gates_before + (GATES * t - 1 if t else 0))
                self.mids = i * (ps.p - 1) + (ps.mids_before + t - 1)
                before = (F_, I_, G_, O_) if t > 1 or (t == 0 and ps.p > 1) else (I_, G_, O_)
                self.read_before = {g: self.gates_before - len(before) + (before.index(g) + 1 if g in before else 0)
                                    for g in self.gates}

        def prev_steps(prev, ps, i):
            if ps.p == 4:
                return prev.steps_before + prev.p * (prev.rounds if isinstance(i, int) and i else
                                                     -(-prev.across // 2)) if isinstance(i, int) else \
                    prev.steps_before + prev.p * prev.rounds
            if ps.p == 3:
                halves = 1 if i * 2 + 1 < ps.across else 2
                return prev.steps_before + prev.p * (prev.rounds // 2 * halves)
            return prev.steps_before + (i + 1) * (2 * ps.nb // (2 * prev.nb)) * prev.p

        def flat(tile, ps):
            return tile[:, 0:ps.cols].rearrange("p (b w) -> p b w", w=ps.nw)

        def nodes_of(states, ps, i, a, t):
            if ps.across == 1:
                batches = states[:, ds((i * 2 + a) * (ps.nb * N), ps.nb * N)]
                return batches.rearrange("p (b n) -> p b n", n=N)[:, :, t:t + (ps.nw - 1) * ps.p + 1:ps.p]
            half, part = divmod(i * 2 + a, ps.across)
            first = part * ps.nw * ps.p + t
            return states[:, half * ps.nb * N:(half + 1) * ps.nb * N].rearrange("p (b n) -> p b n", n=N)[
                :, :, first:first + (ps.nw - 1) * ps.p + 1:ps.p]

        def rounds_of(eng, ps, body):
            if ps.across > 1:
                for i in range(ps.rounds):
                    body(i)
                return
            body(0)
            if ps.rounds > 1:
                with eng.Fori(1, ps.rounds) as i:
                    body(i)

        EB = 2 * GB
        ET = EB * N
        ETURNS = B // EB
        SLOTS = 4

        def slots(name, shape):
            return [sb(f"{name}{i}", shape, side="right", scope=ctx) for i in range(SLOTS)]

        ident_r = sb("ident_r", [128, 128], F32R, side="right", scope=ctx)
        fin, ln3_st, ln3_mv, ln3_ve, ln3_rs, ln3_sh = (slots(n, s) for n, s in (
            ("fin", [N, ET]), ("ln3_st", [N, EB, 6]), ("ln3_mv", [N, EB, 2]), ("ln3_ve", [N, EB]),
            ("ln3_rs", [N, EB]), ("ln3_sh", [N, EB])))
        ident_r_set, sum_mm, st3, mv3, ve3, rs3, rm3, sh3, fin_done = map(sem, (
            "ident_r_set", "sum_mm", "st3", "mv3", "ve3", "rs3", "rm3", "sh3", "fin_done"))
        fin_free = [sem(f"fin_free{i}") for i in range(SLOTS)]
        last_pass = passes[-1]
        gates_total = last_pass.gates_before + last_pass.rounds * last_pass.gates

        assert last_pass.rounds == 2 and last_pass.across == 1

        with nc.Block() as block:
            @block.tensor
            def _(pe):
                for ps in passes:
                    w = [[part[:, ps.p - 1, gate * D:(gate + 1) * D] for gate in range(GATES)]
                         for part in (wih_hi, wih_lo, whh_hi, whh_lo)]
                    out = [[flat(bank[4 * a + gate], ps) for gate in range(GATES)] for a in range(2)]

                    def body(i):
                        if ps.p > 1:
                            prev = passes[ps.p - 2]
                            done = prev_steps(prev, ps, i)
                            for a in range(2):
                                need(pe, h_lo[a], done)
                        for t in range(ps.p):
                            for a in range(2):
                                st = Step(ps, i, t)
                                hi, lo = (nodes_of(s, ps, i, a, t) for s in (st_hi, st_lo))
                                for gate in st.gates:
                                    need(pe, gate_out[a], st.read_before[gate])
                                    pe.matmul(out[a][gate], w[0][gate], hi, start=True, stop=False)
                                    pe.matmul(out[a][gate], w[1][gate], hi, start=False, stop=False)
                                for gate in st.gates:
                                    mm = pe.matmul(out[a][gate], w[0][gate], lo, start=False, stop=st.first)
                                    if st.first:
                                        mm.then_inc(gate_mm[a], 1)
                            if t == 0:
                                continue
                            for a in range(2):
                                st = Step(ps, i, t)
                                hi, lo = flat(mid_hi[a], ps), flat(mid_lo[a], ps)
                                need(pe, h_hi[a], st.n)
                                for gate in st.gates:
                                    pe.matmul(out[a][gate], w[2][gate], hi, start=False, stop=False)
                                    pe.matmul(out[a][gate], w[3][gate], hi, start=False, stop=False)
                                need(pe, h_lo[a], st.n)
                                for gate in st.gates:
                                    pe.matmul(out[a][gate], w[2][gate], lo, start=False, stop=True) \
                                      .then_inc(gate_mm[a], 1)

                    rounds_of(pe, ps, body)

                for g in range(ETURNS):
                    for a in range(2):
                        if g % (ETURNS // 2) == 0:
                            pe.wait_ge(h_lo[a], last_pass.steps_before + last_pass.p * (g // (ETURNS // 2) + 1))
                        if g == a * SLOTS // 2:
                            pe.wait_ge(gate_out[a], gates_total)
                    need(pe, fin_done, g - SLOTS + 1)
                    for half in range(2):
                        out = bank[2 * (g % SLOTS) + half]
                        first = g * EB + half * GB
                        pe.matmul(out[:], ident[:], xres[:, first:first + GB, :].rearrange("p b d -> p (b d)"),
                                  start=True, stop=False)
                        if g == 0 and half == 0:
                            pe.wait_ge(ident_r_set, 1)
                        for b in range(GB):
                            at = slice((first + b) * N, (first + b + 1) * N)
                            for part in (st_hi, st_lo):
                                mm = pe.matmul(out[:, b * D:(b + 1) * D], part[:, at], ident_r[:],
                                               start=False, stop=part is st_lo and b == GB - 1)
                        mm.then_inc(sum_mm, 1)

            @block.scalar
            def _(act):
                tile_of = {I_: act_i, F_: act_f, G_: act_g, O_: act_o}

                def gates_of(ps, st, a):
                    for k, gate in enumerate(st.gates):
                        need(act, gate_mm[a], st.gates_before + k + 1)
                        if gate == O_:
                            need(act, h_full[a], st.n)
                        at = (ps.p - 1) * GATES + gate
                        act.activation(tile_of[gate][a][:, 0:ps.cols], bank[4 * a + gate][:, 0:ps.cols],
                                       ACT.Tanh if gate == G_ else ACT.Sigmoid,
                                       bias=gate_bias[:, at:at + 1]).then_inc(gate_out[a], 1)

                def tanh_of(ps, st, a):
                    need(act, cell_done[a], st.n + 1)
                    need(act, h_lo[a], st.n)
                    act.activation(h_new[a][:, 0:ps.cols], cell[a][:, 0:ps.cols], ACT.Tanh) \
                       .then_inc(tanh_done[a], 1)

                for ps in passes:
                    def body(i):
                        for t in range(ps.p):
                            st = Step(ps, i, t)
                            for a in range(2):
                                gates_of(ps, st, a)
                            for a in range(2):
                                tanh_of(ps, st, a)

                    rounds_of(act, ps, body)

                for u in range(SLOTS):
                    act.sem_inc(fin_free[u], 16)
                with act.Fori(0, ETURNS // SLOTS) as m:
                    for u in range(SLOTS):
                        act.wait_ge(sh3, m * SLOTS + (u + 1))
                        act.wait_ge(fin_free[u], m * 16 + 16)
                        for b in range(EB):
                            at = slice(b % GB * D, (b % GB + 1) * D)
                            op = act.activation(fin[u][:, b * D:(b + 1) * D], bank[2 * u + b // GB][:, at],
                                                ACT.Identity, bias=ln3_sh[u][:, b:b + 1], scale=ln3_rs[u][:, b:b + 1])
                        op.then_inc(fin_done, 1)

            @block.vector
            def _(dve):
                dve.tensor_copy(ident_r[:], ident[:]).then_inc(ident_r_set, 1)

                def cell_of(ps, st, a):
                    c = slice(0, ps.cols)
                    if st.first:
                        need(dve, gate_out[a], st.gates_before + 2)
                        dve.tensor_tensor(cell[a][:, c], act_i[a][:, c], act_g[a][:, c], ALU.mult) \
                           .then_inc(cell_done[a], 1)
                        return
                    need(dve, gate_out[a], st.gates_before + 1)
                    dve.tensor_tensor(fc[a][:, c], act_f[a][:, c], cell[a][:, c], ALU.mult) \
                       .then_inc(cell_ops[a], 1)
                    need(dve, gate_out[a], st.gates_before + 3)
                    dve.tensor_tensor(act_i[a][:, c], act_i[a][:, c], act_g[a][:, c], ALU.mult) \
                       .then_inc(cell_ops[a], 1)
                    need(dve, cell_ops[a], st.mids * 2 + 2)
                    dve.tensor_tensor(cell[a][:, c], act_i[a][:, c], fc[a][:, c], ALU.add) \
                       .then_inc(cell_done[a], 1)

                def state_of(ps, st, a, i):
                    c = slice(0, ps.cols)
                    need(dve, tanh_done[a], st.n + 1)
                    dve.tensor_tensor(nodes_of(st_hi, ps, i, a, st.t) if st.last else flat(mid_hi[a], ps),
                                      flat(act_o[a], ps), flat(h_new[a], ps), ALU.mult).then_inc(h_hi[a], 1)
                    dve.tensor_tensor(h_new[a][:, c], act_o[a][:, c], h_new[a][:, c], ALU.mult) \
                       .then_inc(h_full[a], 1)

                for ps in passes:
                    def body(i):
                        for t in range(ps.p):
                            st = Step(ps, i, t)
                            for a in range(2):
                                cell_of(ps, st, a)
                            for a in range(2):
                                state_of(ps, st, a, i)

                    rounds_of(dve, ps, body)

                with dve.Fori(0, ETURNS // SLOTS) as m:
                    for u in range(SLOTS):
                        g = m * SLOTS + u
                        for b in range(EB):
                            if b % GB == 0:
                                dve.wait_ge(sum_mm, g * 2 + (b // GB + 1))
                            at = slice(b % GB * D, (b % GB + 1) * D)
                            dve.bn_stats(ln3_st[u][:, b, :], bank[2 * u + b // GB][:, at]).then_inc(st3, 1)
                        dve.wait_ge(st3, (g + 1) * EB)
                        dve.memset(idle_words[:, u:u + 1], 0.0)
                        for b in range(EB):
                            dve.bn_aggr(ln3_mv[u][:, b, :], ln3_st[u][:, b, :]).then_inc(mv3, 1)

            @block.gpsimd
            def _(pool):
                for ps in passes:
                    def body(i):
                        for t in range(ps.p):
                            for a in range(2):
                                st = Step(ps, i, t)
                                hi, lo = ((nodes_of(s, ps, i, a, t) for s in (st_hi, st_lo)) if st.last else
                                          (flat(mid_hi[a], ps), flat(mid_lo[a], ps)))
                                need(pool, h_full[a], st.n + 1)
                                pool.tensor_tensor(lo, flat(h_new[a], ps), hi.bitcast(F32), ALU.subtract) \
                                    .then_inc(h_lo[a], 1)

                    rounds_of(pool, ps, body)

                with pool.Fori(0, ETURNS // SLOTS) as m:
                    for u in range(SLOTS):
                        g = m * SLOTS + u
                        mean, var = ln3_mv[u][:, :, 0], ln3_mv[u][:, :, 1]
                        pool.wait_ge(mv3, (g + 1) * EB)
                        pool.tensor_tensor(ln3_ve[u][:], var, eps_wide[:], ALU.add).then_inc(ve3, 1)
                        pool.wait_ge(ve3, g + 1)
                        pool.tensor_tensor(ln3_rs[u][:], ln3_ve[u][:], neg_half_wide[:], ALU.pow).then_inc(rs3, 1)
                        pool.wait_ge(rs3, g + 1)
                        pool.tensor_tensor(ln3_sh[u][:], mean, ln3_rs[u][:], ALU.mult).then_inc(rm3, 1)
                        pool.wait_ge(rm3, g + 1)
                        pool.tensor_tensor(ln3_sh[u][:], zero_wide[:], ln3_sh[u][:], ALU.subtract).then_inc(sh3, 1)

            @block.sync
            def _(sp):
                with sp.Fori(0, ETURNS // SLOTS) as m:
                    for u in range(SLOTS):
                        sp.wait_ge(fin_done, m * SLOTS + (u + 1))
                        sp.dma_start(io["out"][:, ds((m * SLOTS + u) * ET, ET)], fin[u][:]).then_inc(fin_free[u], 16)
                for u in range(SLOTS):
                    sp.wait_ge(fin_free[u], 16 * (1 + ETURNS // SLOTS))


_DRAM = (("x", (N, B * D)), ("xt", (D, TOKENS)), ("adj", (N, N)), ("adjt", (N, N)), ("wqkv", (D, 3 * D)),
         ("w_l1", (D, 3, D)), ("rows", (1, 3, D)), ("w1t", (D, HID * 128)), ("w2t", (128, HID, D)),
         ("wg", (D, 2, D)), ("lstm_w", (D, 2 * STEPS * GATES * D)),
         ("bn1p", (128, 3, HID)), ("bn2p", (128, 3)), ("lstm_b", (D, 2, STEPS * GATES)))


def kernel(**inputs):
    import numpy as np
    import concourse.bacc as bacc
    from concourse.bass_utils import run_bass_kernel_spmd

    a = {k: np.asarray(v) for k, v in inputs.items()}
    cols = lambda v: v.reshape(-1, 128).T
    gates_t = lambda w: w.transpose(2, 0, 1).reshape(D, -1)
    laid = {
        "x": a["x"].transpose(1, 0, 2).reshape(N, B * D),
        "xt": a["x"].transpose(2, 0, 1).reshape(D, TOKENS),
        "adj": a["adj"], "adjt": a["adj"].T, "wqkv": a["L0_gnn_W"],
        "w_l1": a["L1_gnn_W"].transpose(1, 0, 2),
        "rows": np.stack([a["L1_gnn_bias"], a["L3_gnn_bg0"], a["L3_gnn_bg1"]])[None],
        "w1t": a["L2_gnn_W1"].T,
        "w2t": a["L2_gnn_W2"].T.reshape(HID, 128, D).transpose(1, 0, 2),
        "wg": np.stack([a["L3_gnn_Wg0"], a["L3_gnn_Wg1"]], axis=1),
        "lstm_w": np.concatenate([gates_t(a["L3_gnn_Wih"]), gates_t(a["L3_gnn_Whh"])], axis=1),
        "bn1p": np.stack([cols(a[f"L2_gnn_{n}"]) for n in ("b1", "g1", "be1")], axis=1),
        "bn2p": np.concatenate([cols(a[f"L2_gnn_{n}"]) for n in ("b2", "g2", "be2")], axis=1),
        "lstm_b": np.stack([cols(a["L3_gnn_bih"].reshape(-1)), cols(a["L3_gnn_bhh"].reshape(-1))], axis=1),
    }
    laid = {k: np.ascontiguousarray(v) for k, v in laid.items()}

    nc = bacc.Bacc("TRN2", target_bir_lowering=False, num_devices=1)
    io = {n: nc.dram_tensor(f"in_{n}", s, F32, kind="ExternalInput").ap() for n, s in _DRAM}
    io["out"] = nc.dram_tensor("out", (N, B * D), F32, kind="ExternalOutput").ap()
    build(nc, io)
    r = run_bass_kernel_spmd(nc, [{f"in_{n}": v for n, v in laid.items()}], core_ids=[0])
    return np.ascontiguousarray(r.results[0]["out"].reshape(N, B, D).transpose(1, 0, 2))
```

```python
from contextlib import ExitStack

import concourse.bass as bass
from concourse import mybir

F32 = mybir.dt.float32
F32R = mybir.dt.float32r
ALU = mybir.AluOpType
ACT = mybir.ActivationFunctionType
AX_X = mybir.AxisListType.X

B, N, D = 64, 128, 128
HEADS = 4
HD = D // HEADS
VW = HD + 2
GB = 4
G = B // GB
T = GB * N
TOKENS = B * N
HID = 2
STEPS = 4
GATES = 4
EPS = 1e-5
MASKED = -1.0e30


def ds(start, size):
    return bass.ds(start, size)


def need(eng, sem, value):
    if isinstance(value, int) and value <= 0:
        return
    eng.wait_ge(sem, value)


class Turn:

    def __init__(self, m, c, peeled):
        self.m, self.c, self.peeled = m, c, peeled

    def group(self, lag):
        return self.m * 2 + (self.c - lag)

    def half(self, lag):
        return self.m + (self.c - lag) // 2

    def par(self, lag):
        return (self.c - lag) % 2

    def has(self, lag, count=G):
        return not self.peeled or 0 <= self.c - lag < count


def turns(eng, body, first, steady, steady_end, last):
    for c in range(first, steady):
        body(Turn(0, c, True))
    with eng.Fori(0, (steady_end - steady) // 2) as m:
        for u in range(2):
            body(Turn(m, steady + u, False))
    for c in range(steady_end, last):
        body(Turn(0, c, True))


def build(nc, io):
    with ExitStack() as ctx:
        def sb(name, shape, dt=F32, side=None, scope=ctx):
            return scope.enter_context(nc.sbuf_tensor(name, shape, dt, side=side))

        def sem(name):
            return ctx.enter_context(nc.semaphore(name))

        bank = [ctx.enter_context(nc.psum_tensor(f"bank{i}", [128, 512], F32)) for i in range(8)]

        hidden = ctx.enter_context(ExitStack())
        wide0 = sb("wide0", [128, TOKENS], side="right", scope=hidden)
        early = ctx.enter_context(ExitStack())
        wide1 = sb("wide1", [128, TOKENS], side="right", scope=early)
        wqkv = sb("wqkv", [D, 3 * D], side="right", scope=early)
        w_l1 = sb("w_l1", [D, 3, D], side="right", scope=early)
        w1t = sb("w1t", [D, HID * 128], side="right", scope=early)
        w2t = sb("w2t", [128, HID, D], side="right", scope=early)
        wg = sb("wg", [D, 2, D])
        adj = sb("adj", [N, N], side="right", scope=early)
        adjt = sb("adjt", [N, N])
        bn1p = sb("bn1p", [128, 3, HID])
        bn2p = sb("bn2p", [128, 3])
        lstm_b = sb("lstm_b", [D, 2, STEPS * GATES])
        gate_bias = sb("gate_bias", [D, STEPS * GATES])
        rows = sb("rows", [1, 3, D])
        row_bias = sb("row_bias", [128, 3, D])
        ident = sb("ident", [128, 128])
        ones_row = sb("ones_row", [1, 128])
        eps_wide = sb("eps_wide", [128, 2 * GB])
        neg_half_wide = sb("neg_half_wide", [128, 2 * GB])
        eps_tile, neg_half = eps_wide[:, 0:GB], neg_half_wide[:, 0:GB]
        zero_wide = sb("zero_wide", [128, 2 * GB])
        bn_tmp = sb("bn_tmp", [128, HID + 1])
        idle_words = sb("idle_words", [128, 8])
        mask = sb("mask", [N, N], side="right", scope=early)
        adj_split_t = sb("adj_split_t", [N, 3, N], side="right", scope=early)
        ahat_t = sb("ahat_t", [N, N], side="right", scope=early)
        anorm = sb("anorm", [N, N], side="right", scope=early)
        anorm_t = sb("anorm_t", [N, N], side="right", scope=early)
        degs = sb("degs", [N, 8])
        bn_stats1 = sb("bn_stats1", [128, HID, G, 6])
        bn_stats2 = sb("bn_stats2", [128, G, 6])
        bn_fin = sb("bn_fin", [128, 3, 6])

        xres = sb("xres", [N, B, D])
        wide = (wide0, wide1)

        def buffers_of(phase, scope):
            made = []

            def make(*shape):
                made.append(sb(f"{phase}{len(made)}", [128, *shape], side="right", scope=scope))
                return made[-1][:]

            return make

        work_a = ctx.enter_context(ExitStack())
        buffer = buffers_of("a", work_a)
        xt_in = buffer(2, T)
        xg = buffer(2, T)
        qk_full = buffer(T)
        v_one = buffer(2, GB, HEADS * VW)
        scores = buffer(2, HEADS * N)
        neg_max = buffer(2, HEADS)
        probs_t = buffer(2, HEADS * N)
        recip = buffer(HEADS)
        attn = buffer(2, T)
        x1 = buffer(2, T)
        agg3 = buffer(2, 3 * N)
        x2 = buffer(T)
        agg_t = buffer(T)
        ln_st = buffer(2, GB, 6)
        ln_mv = buffer(2, GB, 2)
        ln_rs = buffer(2, GB)

        def halves(name, shape):
            return [sb(f"{name}_{part}", shape, F32R, side="right", scope=work_a) for part in ("hi", "lo")]

        xt_hi, xt_lo = halves("xt", [D, T])
        q_hi, q_lo = halves("q", [D, 2, T])
        k_parts = sb("k_parts", [D, 2, 2, GB // 2 * N], F32R, side="right", scope=work_a)
        k_head = sb("k_head", [D, 2, 2, GB // 2, HEADS, N], F32R, side="right", scope=work_a)
        x1_hi, x1_lo = halves("x1", [N, 2, T])
        agg_hi, agg_lo = halves("agg", [D, T])
        wqk_hi, wqk_lo = halves("wqk", [D, 2 * D])
        w1t_hi, w1t_lo = halves("w1t", [D, HID * 128])
        adj3_hi, adj3_lo = halves("adj3", [N, 3 * N])
        xt_hi_done, xt_lo_done, x1_hi_done, x1_lo_done, g_lo, qk_split, late_split = map(sem, (
            "xt_hi_done", "xt_lo_done", "x1_hi_done", "x1_lo_done", "g_lo", "qk_split", "late_split"))
        q_hi_done, q_lo_done, k_hi_done, k_lo_done = map(sem, ("q_hi_done", "q_lo_done", "k_hi_done", "k_lo_done"))

        xt_ld = [sem(f"xt_ld{i}") for i in range(2)]
        xg_ld = [sem(f"xg_ld{i}") for i in range(2)]
        kh_ld = [sem(f"kh_ld{i}") for i in range(2)]
        bufs_set = sem("bufs_set")
        adj_loaded, wqkv_loaded, rows_loaded, w_l1_loaded, mlp1_loaded, rest_loaded = map(sem, (
            "adj_loaded", "wqkv_loaded", "rows_loaded", "w_l1_loaded", "mlp1_loaded", "rest_loaded"))
        REST_LOADS = 4
        pool_setup = sem("pool_setup")
        dve_setup = sem("dve_setup")
        pe_setup = sem("pe_setup")

        with nc.Block() as block:
            @block.sync
            def _(sp):
                sp.dma_start(adj[:], io["adj"]).then_inc(adj_loaded, 16)
                sp.dma_start(adjt[:], io["adjt"]).then_inc(adj_loaded, 16)
                sp.dma_start(wqkv[:], io["wqkv"]).then_inc(wqkv_loaded, 16)
                sp.dma_start(xt_in[:, 0, :], io["xt"][:, 0:T]).then_inc(xt_ld[0], 16)
                sp.dma_start(rows[:], io["rows"]).then_inc(rows_loaded, 16)
                sp.dma_start(xt_in[:, 1, :], io["xt"][:, T:2 * T]).then_inc(xt_ld[1], 16)
                for g in range(2):
                    sp.dma_start(xg[:, g, :], io["x"][:, g * T:(g + 1) * T]).then_inc(xg_ld[g], 16)
                sp.dma_start(w_l1[:], io["w_l1"]).then_inc(w_l1_loaded, 16)
                for tile, name in ((w1t, "w1t"), (bn1p, "bn1p")):
                    sp.dma_start(tile[:], io[name]).then_inc(mlp1_loaded, 16)
                for tile, name in ((w2t, "w2t"), (bn2p, "bn2p"), (wg, "wg"), (lstm_b, "lstm_b")):
                    sp.dma_start(tile[:], io[name]).then_inc(rest_loaded, 16)

            @block.gpsimd
            def _(pool):
                pool.memset(ident[:], 0.0).then_inc(pool_setup, 1)
                pool.memset(ones_row[:], 1.0).then_inc(pool_setup, 1)
                pool.memset(neg_half_wide[:], -0.5).then_inc(pool_setup, 1)
                pool.memset(eps_wide[:], EPS).then_inc(pool_setup, 1)
                pool.memset(zero_wide[:], 0.0).then_inc(pool_setup, 1)
                pool.wait_ge(pool_setup, 5)
                pool.affine_select(out=ident[:], in_=ident[:], compare_op=ALU.not_equal, fill=1.0, base=0,
                                   pattern=[[-1, N]], channel_multiplier=1).then_inc(pool_setup, 1)
                pool.memset(k_head[:, 1].rearrange("p a b h n -> p (a b h n)").bitcast(F32), 0.0).then_inc(bufs_set, 1)
                pool.wait_ge(adj_loaded, 32)
                pool.affine_select(out=adj_split_t[:, 0, :], in_=adjt[:], compare_op=ALU.is_equal, fill=0.0,
                                   base=0, pattern=[[-1, N]], channel_multiplier=1).then_inc(pool_setup, 1)
                pool.affine_select(out=adj_split_t[:, 1, :], in_=adjt[:], compare_op=ALU.is_gt, fill=0.0,
                                   base=0, pattern=[[-1, N]], channel_multiplier=1).then_inc(pool_setup, 1)
                pool.affine_select(out=adj_split_t[:, 2, :], in_=adjt[:], compare_op=ALU.is_gt, fill=0.0,
                                   base=0, pattern=[[1, N]], channel_multiplier=-1).then_inc(pool_setup, 1)
                pool.wait_ge(xt_hi_done, 1)
                pool.tensor_tensor(xt_lo[:], xt_in[:, 0, :], xt_hi[:].bitcast(F32), ALU.subtract) \
                    .then_inc(xt_lo_done, 1)

            @block.vector
            def _(dve):
                dve.memset(k_head[:, 0].rearrange("p a b h n -> p (a b h n)").bitcast(F32), 0.0).then_inc(bufs_set, 1)
                dve.memset(v_one.rearrange("p a b v -> p (a b v)"), 1.0).then_inc(bufs_set, 1)
                dve.wait_ge(wqkv_loaded, 16)
                dve.tensor_copy(wqk_hi[:], wqkv[:, 0:2 * D]).then_inc(qk_split, 1)
                dve.wait_ge(qk_split, 1)
                dve.tensor_tensor(wqk_lo[:], wqkv[:, 0:2 * D], wqk_hi[:].bitcast(F32), ALU.subtract) \
                   .then_inc(qk_split, 1)

            @block.scalar
            def _(act):
                act.wait_ge(xt_ld[0], 16)
                act.copy(xt_hi[:], xt_in[:, 0, :]).then_inc(xt_hi_done, 1)

        X, P, A, L, Y, H, S = -2, -1, 0, 1, 2, 3, 4

        q_mm, k_mm, v_mm = sem("q_mm"), sem("k_mm"), sem("v_mm")
        q_out, k_out, v_out = sem("q_out"), sem("k_out"), sem("v_out")
        score_mm, score_max, exp_done = sem("score_mm"), sem("score_max"), sem("exp_done")
        pt_mm, pt_out = sem("pt_mm"), sem("pt_out")
        av_mm, av_recip, av_out = sem("av_mm"), sem("av_recip"), sem("av_out")
        s0_done, st0, mv0, ve0, rs0, x1_done, x1_biased = (
            sem("s0_done"), sem("st0"), sem("mv0"), sem("ve0"), sem("rs0"), sem("x1_done"), sem("x1_biased"))
        y_mm, y_out, z_mm = sem("y_mm"), sem("y_out"), sem("z_mm")
        s1_done, st1, mv1, ve1, rs1, x2_done, x2_kept = (
            sem("s1_done"), sem("st1"), sem("mv1"), sem("ve1"), sem("rs1"), sem("x2_done"), sem("x2_kept"))
        g_mm, g_hi, g_out, h_mm, h_out, h_stat = sem("g_mm"), sem("g_hi"), sem("g_out"), sem("h_mm"), sem("h_out"), sem("h_stat")

        def in_halves(a):
            return a.rearrange("p (h x) -> p h x", h=2)

        R0, R1, S0, S1, PTB, OB, YB, ZB = bank
        KH_LOADS = 16 * HEADS

        with nc.Block() as block:
            @block.sync
            def _(sp):
                def load_xt(par, group):
                    sp.dma_start(xt_in[:, par, :], io["xt"][:, ds(group * T, T)]).then_inc(xt_ld[par], 16)

                def load_xg(par, group):
                    sp.dma_start(xg[:, par, :], io["x"][:, ds(group * T, T)]).then_inc(xg_ld[par], 16)

                def scatter(t, half):
                    need(sp, score_mm, (t.group(P) - 1) * GB + (half + 1) * (GB // 2))
                    for h in range(HEADS):
                        rows_h = slice(HD * h, HD * (h + 1))
                        k_rows = k_parts[rows_h, half].rearrange("p a (b n) -> p (a b) n", n=N)
                        blocks = k_head[rows_h, half].rearrange("p a b h n -> p (a b) h n")[:, :, h, :]
                        sp.dma_start(blocks.bitcast(F32), k_rows.bitcast(F32)) \
                          .then_inc(kh_ld[half], 16)

                def turn(t):
                    if t.has(P):
                        sp.wait_ge(bufs_set, 3)
                        need(sp, k_lo_done, t.group(P) + 1)
                        scatter(t, 0)
                        if not t.peeled or t.c - P + 2 < G:
                            need(sp, v_mm, t.group(P) + 1)
                            load_xt(t.par(P), t.group(P) + 2)
                    if t.has(L) and (not t.peeled or t.c - L + 2 < G):
                        need(sp, s0_done, t.group(L) + 1)
                        load_xg(t.par(L), t.group(L) + 2)
                    if t.has(P):
                        scatter(t, 1)

                turns(sp, turn, -1, 3, G - 3, G + 1)

            @block.tensor
            def _(pe):
                pe.wait_ge(wqkv_loaded, 16)
                pe.wait_ge(qk_split, 2)

                def split_product(out, weights, data):
                    for k, (w, x) in enumerate(((0, 0), (1, 0), (0, 1))):
                        mm = pe.matmul(out, weights[w], data[x], start=(k == 0), stop=(k == 2))
                    return mm

                def aggregate(t, j):
                    if t.peeled and t.c == Y and j == 0:
                        pe.wait_ge(late_split, 4)
                        pe.wait_ge(dve_setup, 11)
                    if j % 2 == 0:
                        need(pe, x1_lo_done, t.group(Y) * 2 + (j // 2 + 1))
                    need(pe, y_out, t.group(Y) * GB + j)
                    split_product(YB[:, 0:3 * N],
                                  [part[:, t.par(Y), j * D:(j + 1) * D] for part in (x1_hi, x1_lo)],
                                  (adj3_hi[:], adj3_lo[:])).then_inc(y_mm, 1)

                def turn(t):
                    for j in range(GB):
                        s = t.group(A) * GB + j
                        if t.has(A):
                            if j == 0:
                                need(pe, q_lo_done, t.group(A) + 1)
                            if j % 2 == 0:
                                need(pe, kh_ld[j // 2], (t.group(A) + 1) * KH_LOADS)
                            need(pe, score_max, s - 1)
                            rows_q = slice(j * N, (j + 1) * N)
                            split_product((S0, S1)[j % 2][:],
                                          (q_hi[:, t.par(A), rows_q], q_lo[:, t.par(A), rows_q]),
                                          [k_head[:, j // 2, part, j % 2].rearrange("p h n -> p (h n)")
                                           for part in range(2)]).then_inc(score_mm, 1)
                        if t.has(Y) and j >= 1:
                            aggregate(t, j)
                        lag = A if j >= 1 else L
                        if t.has(lag):
                            need(pe, exp_done, s)
                            need(pe, pt_out, s - 1)
                            for h in range(HEADS):
                                mm = pe.transpose(PTB[:, h * N:(h + 1) * N],
                                                  scores[:, (j + 1) % 2, h * N:(h + 1) * N], ident[:])
                            mm.then_inc(pt_mm, 1)
                        if t.has(Y) and j == 0:
                            aggregate(t, j)
                        if t.has(P):
                            par = t.par(P)
                            if j == 0:
                                need(pe, xt_lo_done, t.group(P) + 1)
                                need(pe, v_out, t.group(P))
                                need(pe, h_out, (t.group(P) - 4) * HID)
                                split_product(R0[:], (wqk_hi[:, 0:D], wqk_lo[:, 0:D]),
                                              (xt_hi[:], xt_lo[:])).then_inc(q_mm, 1)
                            if j == 1:
                                need(pe, k_hi_done, t.group(P))
                                need(pe, h_out, (t.group(P) - 4) * HID)
                                split_product(R1[:], (wqk_hi[:, D:2 * D], wqk_lo[:, D:2 * D]),
                                              (xt_hi[:], xt_lo[:])).then_inc(k_mm, 1)
                            if j == 2:
                                need(pe, q_hi_done, t.group(P) + 1)
                                for b in range(GB):
                                    mm = pe.matmul(R0[:, b * D:(b + 1) * D], xt_in[:, par, b * N:(b + 1) * N],
                                                   wqkv[:, 2 * D:3 * D], start=True, stop=True)
                                mm.then_inc(v_mm, 1)
                        lag = A if j >= 2 else L
                        if t.has(lag):
                            vb = (j - 2) % GB
                            need(pe, pt_out, s - 1)
                            need(pe, av_out, s - 2)
                            need(pe, v_out, t.group(lag) + 1)
                            for h in range(HEADS):
                                mm = pe.matmul(OB[:, h * VW:(h + 1) * VW], probs_t[:, j % 2, h * N:(h + 1) * N],
                                               v_one[:, t.par(lag), vb, h * VW:(h + 1) * VW], start=True, stop=True)
                            mm.then_inc(av_mm, 1)
                        if t.has(H) and j == 2:
                            need(pe, x2_done, t.group(H) + 1)
                            need(pe, h_out, t.group(H) * HID)
                            if t.has(P):
                                need(pe, k_hi_done, t.group(P) + 1)
                            for b in range(GB):
                                mm = pe.matmul(R1[:, b * N:(b + 1) * N], x2[:, b * D:(b + 1) * D],
                                               ahat_t[:], start=True, stop=True)
                            mm.then_inc(g_mm, 1)
                        if t.has(Y):
                            if t.peeled and t.c == Y and j == 0:
                                pe.wait_ge(w_l1_loaded, 16)
                            need(pe, y_out, t.group(Y) * GB + j + 1)
                            if j == 0:
                                need(pe, s1_done, t.group(Y))
                            for k in range(3):
                                mm = pe.matmul(ZB[:, j * D:(j + 1) * D], agg3[:, j % 2, k * N:(k + 1) * N],
                                               w_l1[:, k, :], start=(k == 0), stop=(k == 2))
                            mm.then_inc(z_mm, 1)
                        if t.peeled and t.c == -1 and j == 3:
                            pe.wait_ge(dve_setup, 9)
                            pe.transpose(YB[:, 0:N], anorm[:], ident[:]).then_inc(pe_setup, 1)
                            pe.wait_ge(rows_loaded, 16)
                            pe.matmul(ZB[:, 0:3 * D], ones_row[:], rows[:].rearrange("p a d -> p (a d)"),
                                      start=True, stop=True).then_inc(pe_setup, 1)
                        if t.has(H) and j == 3:
                            need(pe, g_lo, t.group(H) + 1)
                            need(pe, h_out, t.group(H) * HID)
                            if t.has(P):
                                need(pe, v_out, t.group(P) + 1)
                            for k, out in enumerate((R0, R1)):
                                cols = slice(k * 128, (k + 1) * 128)
                                split_product(out[:], (w1t_hi[:, cols], w1t_lo[:, cols]),
                                              (agg_hi[:], agg_lo[:])).then_inc(h_mm, 1)

                turns(pe, turn, -1, 4, G - 2, G + 3)

            @block.scalar
            def _(act):
                def turn(t):
                    for j in range(GB):
                        s = t.group(A) * GB + j
                        if t.has(Y):
                            y = t.group(Y) * GB + j
                            need(act, y_mm, y + 1)
                            need(act, z_mm, y - 1)
                            act.copy(agg3[:, j % 2, :], YB[:, 0:3 * N]).then_inc(y_out, 1)
                        if t.has(P) and j == 0:
                            need(act, q_mm, t.group(P) + 1)
                            need(act, k_lo_done, t.group(P))
                            act.mul(qk_full, R0[:], HD ** -0.5).then_inc(q_out, 1)
                            need(act, score_mm, (t.group(P) - 1) * GB)
                            act.mul(q_hi[:, t.par(P), :], R0[:], HD ** -0.5).then_inc(q_hi_done, 1)
                        if t.has(P) and j == 1:
                            need(act, k_mm, t.group(P) + 1)
                            need(act, q_lo_done, t.group(P) + 1)
                            act.copy(qk_full, R1[:]).then_inc(k_out, 1)
                            for half in range(2):
                                need(act, kh_ld[half], t.group(P) * KH_LOADS)
                            act.copy(k_parts[:, :, 0, :], in_halves(R1[:])).then_inc(k_hi_done, 1)
                        if t.has(A):
                            need(act, score_max, s + 1)
                            for h in range(HEADS):
                                e = act.activation(scores[:, j % 2, h * N:(h + 1) * N],
                                                   scores[:, j % 2, h * N:(h + 1) * N], ACT.Exp,
                                                   bias=neg_max[:, j % 2, h:h + 1], scale=-1.0)
                            e.then_inc(exp_done, 1)
                        if t.has(X) and j == 2:
                            need(act, xt_ld[t.par(X)], (t.half(X) + 1) * 16)
                            need(act, k_mm, t.group(X))
                            act.copy(xt_hi[:], xt_in[:, t.par(X), :]).then_inc(xt_hi_done, 1)
                        if t.has(H) and j == 2:
                            need(act, g_mm, t.group(H) + 1)
                            need(act, h_mm, t.group(H) * HID)
                            act.copy(agg_hi[:], R1[:]).then_inc(g_hi, 1)
                            act.copy(agg_t, R1[:]).then_inc(g_out, 1)
                        if t.has(L) and j == 3:
                            need(act, x1_done, t.group(L) + 1)
                            need(act, y_mm, (t.group(L) - 1) * GB)
                            for half in range(2):
                                cols = slice(half * (T // 2), (half + 1) * (T // 2))
                                act.copy(x1_hi[:, t.par(L), cols], x1[:, t.par(L), cols]).then_inc(x1_hi_done, 1)
                        if t.has(H) and j == 3:
                            for k, src in enumerate((R0, R1)):
                                need(act, h_mm, t.group(H) * HID + k + 1)
                                act.activation(wide[k][:, ds(t.group(H) * T, T)], src[:], ACT.Identity,
                                               bias=bn1p[:, 0, k:k + 1]).then_inc(h_out, 1)

                turns(act, turn, -1, 5, G - 3, G + 3)

            @block.vector
            def _(dve):
                dve.wait_ge(adj_loaded, 32)
                dve.tensor_scalar(mask[:], adj[:], 0.0, MASKED, ALU.is_equal, ALU.mult).then_inc(dve_setup, 1)
                dve.wait_ge(pool_setup, 9)
                dve.tensor_tensor(anorm[:], adj[:], ident[:], ALU.add).then_inc(dve_setup, 1)
                dve.tensor_tensor(anorm_t[:], adjt[:], ident[:], ALU.add).then_inc(dve_setup, 1)
                dve.tensor_reduce(degs[:, 2:3], adj_split_t[:, 0, :], AX_X, ALU.add).then_inc(dve_setup, 1)
                dve.wait_ge(dve_setup, 4)
                dve.tensor_reduce(degs[:, 0:1], anorm[:], AX_X, ALU.add).then_inc(dve_setup, 1)
                dve.tensor_reduce(degs[:, 1:2], anorm_t[:], AX_X, ALU.add).then_inc(dve_setup, 1)
                dve.wait_ge(dve_setup, 6)
                dve.tensor_tensor(degs[:, 3:4], degs[:, 0:1], degs[:, 1:2], ALU.add).then_inc(dve_setup, 1)
                dve.wait_ge(dve_setup, 7)
                dve.scalar_tensor_tensor(degs[:, 4:5], degs[:, 3:4], -1.0, degs[:, 2:3],
                                         ALU.add, ALU.subtract).then_inc(dve_setup, 1)
                dve.wait_ge(pool_setup, 10)
                dve.tensor_scalar(anorm[:], anorm[:], degs[:, 5:6], None, ALU.mult).then_inc(dve_setup, 1)
                dve.wait_ge(dve_setup, 1)

                def carry_waits(word):
                    dve.memset(idle_words[:, word:word + 1], 0.0)

                def ln_stats(i, src, stat_sem, mv_sem, group):
                    for b in range(GB):
                        dve.bn_stats(ln_st[:, i, b, :], src[:, b * D:(b + 1) * D]).then_inc(stat_sem, 1)
                    need(dve, stat_sem, (group + 1) * GB)
                    carry_waits(GB + i)
                    for b in range(GB):
                        dve.bn_aggr(ln_mv[:, i, b, :], ln_st[:, i, b, :]).then_inc(mv_sem, 1)

                def ln_apply(i, src, dst, done):
                    for b in range(GB):
                        op = dve.tensor_scalar(dst[:, b * D:(b + 1) * D], src[:, b * D:(b + 1) * D],
                                               ln_mv[:, i, b, 0:1], ln_rs[:, i, b:b + 1], ALU.subtract, ALU.mult)
                    op.then_inc(done, 1)

                def turn(t):
                    for j in range(GB):
                        s = t.group(A) * GB + j
                        if t.has(H) and j == 0:
                            need(dve, z_mm, (t.group(H) + 1) * GB)
                            need(dve, x1_biased, t.group(H) + 1)
                            dve.tensor_tensor(x1[:, t.par(H), :], ZB[:], x1[:, t.par(H), :], ALU.add) \
                               .then_inc(s1_done, 1)
                        if t.has(A):
                            need(dve, score_mm, s + 1)
                            need(dve, pt_mm, s - 1)
                            carry_waits(j)
                            for h in range(HEADS):
                                cols = slice(h * N, (h + 1) * N)
                                op = dve.tensor_tensor_reduce(scores[:, j % 2, cols], (S0, S1)[j % 2][:, cols], mask[:],
                                                              -1.0, 3.0e38, ALU.add, ALU.min,
                                                              neg_max[:, j % 2, h:h + 1])
                            op.then_inc(score_max, 1)
                        if t.has(A if j >= 1 else L):
                            need(dve, pt_mm, s)
                            need(dve, av_mm, s - 2)
                            dve.tensor_copy(probs_t[:, (j + 1) % 2, :], PTB[:]).then_inc(pt_out, 1)
                        if t.has(P) and j == 2:
                            need(dve, v_mm, t.group(P) + 1)
                            need(dve, av_mm, (t.group(P) - 1) * GB)
                            dve.tensor_copy(
                                v_one[:, t.par(P), :, :].rearrange("p b (h v) -> p (b h) v", v=VW)[:, :, 0:HD],
                                R0[:].rearrange("p (c v) -> p c v", v=HD)).then_inc(v_out, 1)
                        lag = A if j >= 2 else L
                        if t.has(lag):
                            o = OB[:, 0:HEADS * VW].rearrange("p (h v) -> p h v", v=VW)
                            need(dve, av_mm, s - 1)
                            dve.reciprocal(recip, o[:, :, HD]).then_inc(av_recip, 1)
                            need(dve, av_recip, s - 1)
                            b = (j - 2) % GB
                            dve.tensor_tensor(
                                attn[:, t.par(lag), b * D:(b + 1) * D].rearrange("p (h v) -> p h v", v=HD),
                                o[:, :, 0:HD], recip.unsqueeze(2).broadcast_to([N, HEADS, HD]),
                                ALU.mult).then_inc(av_out, 1)
                        if t.has(H) and j == 0:
                            need(dve, s1_done, t.group(H) + 1)
                            need(dve, ve1, t.group(H))
                            ln_stats(1, x1[:, t.par(H), :], st1, mv1, t.group(H))
                        if t.has(S) and j == 0:
                            for k in range(HID):
                                need(dve, h_out, t.group(S) * HID + k + 1)
                                dve.bn_stats(bn_stats1[:, k, ds(t.group(S), 1), :].rearrange("p a s -> p (a s)"),
                                             wide[k][:, ds(t.group(S) * T, T)]).then_inc(h_stat, 1)
                        if t.has(H) and j == 1:
                            need(dve, rs1, t.group(H) + 1)
                            need(dve, g_mm, t.group(H))
                            need(dve, x2_kept, t.group(H))
                            ln_apply(1, x1[:, t.par(H), :], x2, x2_done)
                        if t.has(L) and j == 2:
                            need(dve, s0_done, t.group(L) + 1)
                            ln_stats(0, attn[:, t.par(L), :], st0, mv0, t.group(L))
                        if t.peeled and t.c == -1 and j == 3:
                            dve.wait_ge(pe_setup, 1)
                            dve.tensor_scalar(ahat_t[:], YB[:, 0:N], degs[:, 5:6], None, ALU.mult) \
                               .then_inc(dve_setup, 1)
                            dve.wait_ge(pe_setup, 2)
                            dve.tensor_copy(row_bias[:], ZB[:, 0:3 * D].rearrange("p (a d) -> p a d", a=3)) \
                               .then_inc(dve_setup, 1)
                        if t.has(L) and j == 3:
                            need(dve, rs0, t.group(L) + 1)
                            need(dve, x1_biased, t.group(L) - 1)
                            ln_apply(0, attn[:, t.par(L), :], x1[:, t.par(L), :], x1_done)

                turns(dve, turn, -1, 6, G - 2, G + 4)

            @block.gpsimd
            def _(pool):
                pool.wait_ge(dve_setup, 8)
                pool.tensor_tensor(degs[:, 5:6], degs[:, 4:5], neg_half[:, 0:1], ALU.pow).then_inc(pool_setup, 1)

                def rstd(i, mv_sem, eps_sem, done, group):
                    need(pool, mv_sem, (group + 1) * GB)
                    pool.tensor_tensor(ln_rs[:, i, :], ln_mv[:, i, :, 1], eps_tile, ALU.add).then_inc(eps_sem, 1)
                    need(pool, eps_sem, group + 1)
                    pool.tensor_tensor(ln_rs[:, i, :], ln_rs[:, i, :], neg_half, ALU.pow).then_inc(done, 1)

                def turn(t):
                    if t.has(P):
                        need(pool, q_hi_done, t.group(P) + 1)
                        pool.tensor_tensor(q_lo[:, t.par(P), :], qk_full, q_hi[:, t.par(P), :].bitcast(F32),
                                           ALU.subtract).then_inc(q_lo_done, 1)
                    if t.has(H):
                        need(pool, x2_done, t.group(H))
                        rstd(1, mv1, ve1, rs1, t.group(H))
                    if t.has(P):
                        need(pool, k_hi_done, t.group(P) + 1)
                        pool.tensor_tensor(k_parts[:, :, 1, :], in_halves(qk_full), k_parts[:, :, 0, :].bitcast(F32),
                                           ALU.subtract).then_inc(k_lo_done, 1)
                    if t.has(L):
                        need(pool, av_out, (t.group(L) + 1) * GB)
                        need(pool, xg_ld[t.par(L)], (t.half(L) + 1) * 16)
                        pool.tensor_tensor(attn[:, t.par(L), :], attn[:, t.par(L), :], xg[:, t.par(L), :],
                                           ALU.add).then_inc(s0_done, 1)
                    if t.has(H):
                        need(pool, x2_done, t.group(H) + 1)
                        pool.tensor_copy(xres[:, ds(t.group(H) * GB, GB), :].rearrange("p b d -> p (b d)"),
                                         x2).then_inc(x2_kept, 1)
                    if t.has(L):
                        rstd(0, mv0, ve0, rs0, t.group(L))
                    if t.peeled and t.c == 0:
                        pool.wait_ge(mlp1_loaded, 32)
                        adj3 = adj_split_t[:].rearrange("p a n -> p (a n)")
                        pool.tensor_copy(adj3_hi[:], adj3).then_inc(late_split, 1)
                        pool.tensor_copy(w1t_hi[:], w1t[:]).then_inc(late_split, 1)
                        pool.wait_ge(late_split, 2)
                        pool.tensor_tensor(adj3_lo[:], adj3, adj3_hi[:].bitcast(F32), ALU.subtract) \
                            .then_inc(late_split, 1)
                        pool.tensor_tensor(w1t_lo[:], w1t[:], w1t_hi[:].bitcast(F32), ALU.subtract) \
                            .then_inc(late_split, 1)
                    if t.has(H):
                        need(pool, g_out, t.group(H) + 1)
                        pool.tensor_tensor(agg_lo[:], agg_t, agg_hi[:].bitcast(F32), ALU.subtract).then_inc(g_lo, 1)
                    if t.has(X):
                        need(pool, xt_hi_done, t.group(X) + 1)
                        pool.tensor_tensor(xt_lo[:], xt_in[:, t.par(X), :], xt_hi[:].bitcast(F32), ALU.subtract) \
                            .then_inc(xt_lo_done, 1)
                    if t.has(L):
                        for half in range(2):
                            cols = slice(half * (T // 2), (half + 1) * (T // 2))
                            need(pool, x1_hi_done, t.group(L) * 2 + (half + 1))
                            pool.tensor_tensor(x1_lo[:, t.par(L), cols], x1[:, t.par(L), cols],
                                               x1_hi[:, t.par(L), cols].bitcast(F32), ALU.subtract) \
                                .then_inc(x1_lo_done, 1)
                        if t.peeled and t.c == L:
                            pool.wait_ge(dve_setup, 11)
                        need(pool, x1_lo_done, t.group(L) * 2 + 2)
                        pool.tensor_tensor(x1[:, t.par(L), :].rearrange("p (b d) -> p b d", d=D),
                                           x1[:, t.par(L), :].rearrange("p (b d) -> p b d", d=D),
                                           row_bias[:, 0:1, :].broadcast_to([N, GB, D]),
                                           ALU.add).then_inc(x1_biased, 1)

                turns(pool, turn, -1, 5, G - 3, G + 3)

        work_a.close()
        wih_hi, wih_lo, whh_hi, whh_lo = (
            sb(n, [D, STEPS, GATES * D], F32R) for n in ("wih_hi", "wih_lo", "whh_hi", "whh_lo"))
        work_b = ctx.enter_context(ExitStack())
        buffer = buffers_of("b", work_b)
        hid = buffer(2, HID, T)
        stage = sb("stage", [D, 2 * STEPS * GATES * D], side="right", scope=work_b)
        stage_loaded = sem("stage_loaded")
        bn_eps, bn_rstd, bn_dve, w_split = sem("bn_eps"), sem("bn_rstd"), sem("bn_dve"), sem("w_split")
        bias_sum = sem("bias_sum")
        relu_done, mlp_mm, y2_out, y2_stat = sem("relu_done"), sem("mlp_mm"), sem("y2_out"), sem("y2_stat")

        def bn_finish_dve(dve, slots, stats, gain, offset, before):
            f = bn_fin[:, slots, :]
            for k, st in enumerate(stats):
                dve.bn_aggr(f[:, k, 0:2], st).then_inc(bn_dve, 1)
            before += len(stats)
            dve.wait_ge(bn_rstd, 1 if slots.start == 0 else 2)
            dve.tensor_tensor(f[:, :, 4], f[:, :, 3], gain, ALU.mult).then_inc(bn_dve, 1)
            dve.wait_ge(bn_dve, before + 1)
            dve.tensor_tensor(bn_tmp[:, slots], f[:, :, 0], f[:, :, 4], ALU.mult).then_inc(bn_dve, 1)
            dve.wait_ge(bn_dve, before + 2)
            dve.tensor_tensor(f[:, :, 5], offset, bn_tmp[:, slots], ALU.subtract).then_inc(bn_dve, 1)

        def bn_finish_pool(pool, slots, blocks, before):
            f = bn_fin[:, slots, :]
            n = 1 if slots.start == 0 else 2
            pool.wait_ge(bn_dve, before + blocks)
            pool.tensor_tensor(f[:, :, 2], f[:, :, 1], eps_tile[:, 0:blocks], ALU.add).then_inc(bn_eps, 1)
            pool.wait_ge(bn_eps, n)
            pool.tensor_tensor(f[:, :, 3], f[:, :, 2], neg_half[:, 0:blocks], ALU.pow).then_inc(bn_rstd, 1)

        MLP1, MLP2 = slice(0, HID), slice(HID, HID + 1)
        BN1_OPS = HID + 3

        with nc.Block() as block:
            @block.vector
            def _(dve):
                bn_finish_dve(dve, MLP1, [bn_stats1[:, k, :, :].rearrange("p g s -> p (g s)") for k in range(HID)],
                              bn1p[:, 1, :], bn1p[:, 2, :], 0)
                dve.wait_ge(rest_loaded, 16 * REST_LOADS)
                dve.tensor_tensor(gate_bias[:], lstm_b[:, 0, :], lstm_b[:, 1, :], ALU.add).then_inc(bias_sum, 1)

                def turn(t):
                    g = t.group(0)
                    cols = ds(g * T, T)
                    need(dve, mlp_mm, g + 1)
                    dve.tensor_scalar(wide0[:, cols], bank[t.par(0)][:], bn2p[:, 0:1], None, ALU.add) \
                       .then_inc(y2_out, 1)
                    need(dve, y2_out, g + 1)
                    dve.bn_stats(bn_stats2[:, ds(g, 1), :].rearrange("p a s -> p (a s)"), wide0[:, cols]) \
                       .then_inc(y2_stat, 1)

                turns(dve, turn, 0, 2, G, G)

            @block.sync
            def _(sp):
                sp.dma_start(stage[:], io["lstm_w"]).then_inc(stage_loaded, 16)

            @block.gpsimd
            def _(pool):
                bn_finish_pool(pool, MLP1, HID, 0)
                pool.wait_ge(stage_loaded, 16)
                for n, (hi, lo) in enumerate(((wih_hi, wih_lo), (whh_hi, whh_lo))):
                    raw = stage[:, n * STEPS * GATES * D:(n + 1) * STEPS * GATES * D]
                    pool.tensor_copy(hi[:].rearrange("k s g -> k (s g)"), raw).then_inc(w_split, 1)
                    pool.wait_ge(w_split, 2 * n + 1)
                    pool.tensor_tensor(lo[:].rearrange("k s g -> k (s g)"), raw,
                                       hi[:].rearrange("k s g -> k (s g)").bitcast(F32),
                                       ALU.subtract).then_inc(w_split, 1)

            @block.scalar
            def _(act):
                act.wait_ge(bn_dve, BN1_OPS)

                def turn(t):
                    g = t.group(0)
                    need(act, mlp_mm, g - 1)
                    for k in range(HID):
                        act.activation(hid[:, t.par(0), k, :], wide[k][:, ds(g * T, T)], ACT.Relu,
                                       bias=bn_fin[:, k, 5:6], scale=bn_fin[:, k, 4:5]).then_inc(relu_done, 1)

                turns(act, turn, 0, 2, G, G)

            @block.tensor
            def _(pe):
                pe.wait_ge(rest_loaded, 16 * REST_LOADS)

                def turn(t):
                    g = t.group(0)
                    need(pe, y2_out, g - 1)
                    for k in range(HID):
                        need(pe, relu_done, g * HID + k + 1)
                        mm = pe.matmul(bank[t.par(0)][:], w2t[:, k, :], hid[:, t.par(0), k, :],
                                       start=(k == 0), stop=(k == HID - 1))
                    mm.then_inc(mlp_mm, 1)

                turns(pe, turn, 0, 2, G, G)

        work_b.close()
        early.close()
        st_hi, st_lo = sb("st_hi", [D, TOKENS], F32R), sb("st_lo", [D, TOKENS], F32R)
        work_c = ctx.enter_context(ExitStack())
        buffer = buffers_of("c", work_c)
        y_bn = buffer(2, T)
        s2 = buffer(2, T)
        x3 = buffer(2, T)
        x3_t = buffer(T)
        u0 = buffer(T)
        v0 = buffer(T)
        u1 = buffer(T)
        v1 = buffer(T)
        ln2_st = buffer(2, GB, 6)
        ln2_mv = buffer(2, GB, 2)
        ln2_ve = buffer(2, GB)
        ln2_rs = buffer(2, GB)
        ln2_sh = buffer(2, GB)
        BT, XT, U0, V0, U1, V1 = bank[0:6]
        ybn_done, bt_mm, s2_done, st2, mv2, ve2, rs2 = (
            sem("ybn_done"), sem("bt_mm"), sem("s2_done"), sem("st2"), sem("mv2"), sem("ve2"), sem("rs2"))
        rm2, sh2, x3_dve, x3_act = sem("rm2"), sem("sh2"), sem("x3_dve"), sem("x3_act")
        x3_kept = [sem(f"x3_kept{i}") for i in range(2)]
        xt_mm, xt_out = sem("xt_mm"), sem("xt_out")
        u0_mm, u0_out, v0_mm, v0_out = sem("u0_mm"), sem("u0_out"), sem("v0_mm"), sem("v0_out")
        u1_mm, u1_out, v1_mm, v1_out = sem("u1_mm"), sem("u1_out"), sem("v1_mm"), sem("v1_out")
        v1_hi, v1_lo = sem("v1_hi"), sem("v1_lo")

        def by_batch(a):
            return a.rearrange("p (b d) -> p b d", d=D)

        with nc.Block() as block:
            @block.tensor
            def _(pe):
                def four(out, lhs, rhs, done):
                    for b in range(GB):
                        cols = slice(b * 128, (b + 1) * 128)
                        if rhs is None:
                            mm = pe.transpose(out[:, cols], lhs[:, cols], ident[:])
                        else:
                            mm = pe.matmul(out[:, cols], lhs[:, cols], rhs, start=True, stop=True)
                    mm.then_inc(done, 1)

                def turn(t):
                    if t.has(3):
                        need(pe, xt_out, t.group(3) + 1)
                        need(pe, u0_out, t.group(3))
                        four(U0, x3_t, wg[:, 0, :], u0_mm)
                    if t.has(0):
                        need(pe, ybn_done, t.group(0) + 1)
                        need(pe, s2_done, t.group(0))
                        four(BT, y_bn[:, t.par(0), :], None, bt_mm)
                    if t.has(4):
                        need(pe, v0_out, t.group(4) + 1)
                        need(pe, u1_out, t.group(4))
                        four(U1, v0, wg[:, 1, :], u1_mm)
                    if t.has(2):
                        need(pe, x3_dve, t.group(2) + 1)
                        need(pe, x3_act, t.group(2) + 1)
                        need(pe, xt_out, t.group(2))
                        four(XT, x3[:, t.par(2), :], None, xt_mm)
                    if t.has(3):
                        need(pe, u0_out, t.group(3) + 1)
                        need(pe, v0_out, t.group(3))
                        four(V0, u0, adjt[:], v0_mm)
                    if t.has(4):
                        need(pe, u1_out, t.group(4) + 1)
                        need(pe, v1_out, t.group(4))
                        four(V1, u1, adjt[:], v1_mm)

                turns(pe, turn, 0, 6, G, G + 4)

            def x3_free(eng, t):
                need(eng, xt_mm, t.group(1) - 1)
                if not t.peeled or t.c - 1 >= 2:
                    need(eng, x3_kept[t.par(1)], t.half(1) * 16)

            ON_ACT = 2

            @block.scalar
            def _(act):
                act.wait_ge(bn_dve, BN1_OPS + 4)

                def turn(t):
                    if t.has(5):
                        need(act, v1_mm, t.group(5) + 1)
                        act.activation(st_hi[:, ds(t.group(5) * T, T)], V1[:], ACT.Relu).then_inc(v1_hi, 1)
                        need(act, v1_lo, t.group(5))
                        act.activation(v1, V1[:], ACT.Relu).then_inc(v1_out, 1)
                    if t.has(-1):
                        need(act, bt_mm, t.group(-1) - 1)
                        act.activation(y_bn[:, t.par(-1), :], wide0[:, ds(t.group(-1) * T, T)], ACT.Identity,
                                       bias=bn_fin[:, HID, 5:6], scale=bn_fin[:, HID, 4:5]).then_inc(ybn_done, 1)
                    if t.has(1):
                        need(act, sh2, t.group(1) + 1)
                        x3_free(act, t)
                        p = t.par(1)
                        for b in range(GB - ON_ACT, GB):
                            op = act.activation(x3[:, p, b * D:(b + 1) * D], s2[:, p, b * D:(b + 1) * D],
                                                ACT.Identity, bias=ln2_sh[:, p, b:b + 1], scale=ln2_rs[:, p, b:b + 1])
                        op.then_inc(x3_act, 1)
                    if t.has(2):
                        need(act, xt_mm, t.group(2) + 1)
                        need(act, u0_mm, t.group(2))
                        act.copy(x3_t, XT[:]).then_inc(xt_out, 1)
                    if t.has(3):
                        need(act, v0_mm, t.group(3) + 1)
                        need(act, u1_mm, t.group(3))
                        act.activation(v0, V0[:], ACT.Relu).then_inc(v0_out, 1)

                turns(act, turn, -1, 7, G - 1, G + 5)

            @block.vector
            def _(dve):
                bn_finish_dve(dve, MLP2, [bn_stats2[:].rearrange("p g s -> p (g s)")], bn2p[:, 1:2], bn2p[:, 2:3],
                              BN1_OPS)

                def turn(t):
                    p = t.par(0)
                    if t.has(3):
                        need(dve, u0_mm, t.group(3) + 1)
                        need(dve, v0_mm, t.group(3))
                        dve.tensor_tensor(by_batch(u0), by_batch(U0[:]), row_bias[:, 1:2, :].broadcast_to([N, GB, D]),
                                          ALU.add).then_inc(u0_out, 1)
                    if t.has(0):
                        g = t.group(0)
                        need(dve, bt_mm, g + 1)
                        need(dve, x3_act, g - 1)
                        dve.tensor_tensor(by_batch(s2[:, p, :]), by_batch(BT[:]), xres[:, ds(g * GB, GB), :],
                                          ALU.add).then_inc(s2_done, 1)
                    if t.has(4):
                        need(dve, u1_mm, t.group(4) + 1)
                        need(dve, v1_mm, t.group(4))
                        dve.tensor_tensor(by_batch(u1), by_batch(U1[:]), row_bias[:, 2:3, :].broadcast_to([N, GB, D]),
                                          ALU.add).then_inc(u1_out, 1)
                    if t.has(1):
                        q = t.par(1)
                        need(dve, rs2, t.group(1) + 1)
                        x3_free(dve, t)
                        for b in range(GB - ON_ACT):
                            op = dve.tensor_scalar(x3[:, q, b * D:(b + 1) * D], s2[:, q, b * D:(b + 1) * D],
                                                   ln2_mv[:, q, b, 0:1], ln2_rs[:, q, b:b + 1], ALU.subtract, ALU.mult)
                        op.then_inc(x3_dve, 1)
                    if t.has(0):
                        need(dve, s2_done, t.group(0) + 1)
                        for b in range(GB):
                            dve.bn_stats(ln2_st[:, p, b, :], s2[:, p, b * D:(b + 1) * D]).then_inc(st2, 1)
                        need(dve, st2, (t.group(0) + 1) * GB)
                        need(dve, sh2, t.group(0) - 1)
                        dve.memset(idle_words[:, p:p + 1], 0.0)
                        for b in range(GB):
                            dve.bn_aggr(ln2_mv[:, p, b, :], ln2_st[:, p, b, :]).then_inc(mv2, 1)

                turns(dve, turn, 0, 6, G, G + 4)

            @block.gpsimd
            def _(pool):
                bn_finish_pool(pool, MLP2, 1, BN1_OPS)

                def turn(t):
                    if t.has(5):
                        cols = ds(t.group(5) * T, T)
                        need(pool, v1_out, t.group(5) + 1)
                        pool.tensor_tensor(st_lo[:, cols], v1, st_hi[:, cols].bitcast(F32), ALU.subtract) \
                            .then_inc(v1_lo, 1)
                    if t.has(0):
                        g, p = t.group(0), t.par(0)
                        need(pool, mv2, (g + 1) * GB)
                        pool.tensor_tensor(ln2_ve[:, p, :], ln2_mv[:, p, :, 1], eps_tile, ALU.add).then_inc(ve2, 1)
                        need(pool, ve2, g + 1)
                        need(pool, x3_dve, g - 1)
                        need(pool, x3_act, g - 1)
                        pool.tensor_tensor(ln2_rs[:, p, :], ln2_ve[:, p, :], neg_half, ALU.pow).then_inc(rs2, 1)
                        need(pool, rs2, g + 1)
                        pool.tensor_tensor(ln2_sh[:, p, :], ln2_mv[:, p, :, 0], ln2_rs[:, p, :], ALU.mult) \
                            .then_inc(rm2, 1)
                        need(pool, rm2, g + 1)
                        pool.tensor_tensor(ln2_sh[:, p, :], zero_wide[:, 0:GB], ln2_sh[:, p, :], ALU.subtract) \
                            .then_inc(sh2, 1)
                turns(pool, turn, 0, 6, G, G + 5)

            @block.sync
            def _(sp):
                def turn(t):
                    g = t.group(0)
                    need(sp, x3_dve, g + 1)
                    need(sp, x3_act, g + 1)
                    sp.dma_start(xres[:, ds(g * GB, GB), :], by_batch(x3[:, t.par(0), :])) \
                        .then_inc(x3_kept[t.par(0)], 16)

                turns(sp, turn, 0, 2, G, G)
                for par in range(2):
                    sp.wait_ge(x3_kept[par], 16 * (G // 2))

        work_c.close()
        hidden.close()
        C = 512
        I_, F_, G_, O_ = range(GATES)

        def tiles(name, shape, dt=F32):
            return [sb(f"{name}{a}", shape, dt, side="right") for a in range(2)]

        mid_hi, mid_lo = tiles("mid_hi", [D, C], F32R), tiles("mid_lo", [D, C], F32R)
        act_i, act_f, act_g, act_o, cell, fc, h_new = (
            tiles(n, [D, C]) for n in ("act_i", "act_f", "act_g", "act_o", "cell", "fc", "h_new"))

        def pair(name):
            return [sem(f"{name}{a}") for a in range(2)]

        gate_mm, gate_out, cell_ops, cell_done, tanh_done, h_full, h_hi, h_lo = map(pair, (
            "gate_mm", "gate_out", "cell_ops", "cell_done", "tanh_done", "h_full", "h_hi", "h_lo"))

        class Pass:
            pass

        passes = []
        steps_before = gates_before = mids_before = 0
        for p, (nb, nw) in {1: (GB, N), 2: (8, 64), 3: (32, 14), 4: (16, 32)}.items():
            ps = Pass()
            ps.p, ps.nb, ps.nw, ps.cols = p, nb, nw, nb * nw
            ps.across = (N // p) // nw
            ps.rounds = (B // nb) * ps.across // 2
            ps.steps_before, ps.gates_before, ps.mids_before = steps_before, gates_before, mids_before
            ps.gates = 3 + GATES * (p - 1)
            steps_before += ps.rounds * p
            gates_before += ps.rounds * ps.gates
            mids_before += ps.rounds * (p - 1)
            assert ps.across * nw == N // p and ps.cols <= C
            passes.append(ps)

        class Step:

            def __init__(self, ps, i, t):
                self.ps, self.t, self.first, self.last = ps, t, t == 0, t == ps.p - 1
                self.gates = (I_, G_, O_) if self.first else (F_, I_, G_, O_)
                self.n = i * ps.p + (ps.steps_before + t)
                self.gates_before = i * ps.gates + (ps.gates_before + (GATES * t - 1 if t else 0))
                self.mids = i * (ps.p - 1) + (ps.mids_before + t - 1)
                before = (F_, I_, G_, O_) if t > 1 or (t == 0 and ps.p > 1) else (I_, G_, O_)
                self.read_before = {g: self.gates_before - len(before) + (before.index(g) + 1 if g in before else 0)
                                    for g in self.gates}

        def prev_steps(prev, ps, i):
            if isinstance(i, int):
                batches = ((i * 2 + 1) // ps.across + 1) * ps.nb
                rounds = -(-(batches // prev.nb * prev.across) // 2)
            elif prev.across == 1:
                rounds = (i + 1) * (ps.nb // prev.nb)
            else:
                rounds = prev.rounds
            return rounds * prev.p + prev.steps_before

        def flat(tile, ps):
            return tile[:, 0:ps.cols].rearrange("p (b w) -> p b w", w=ps.nw)

        def nodes_of(states, ps, i, a, t):
            if ps.across == 1:
                batches = states[:, ds((i * 2 + a) * (ps.nb * N), ps.nb * N)]
                return batches.rearrange("p (b n) -> p b n", n=N)[:, :, t:t + (ps.nw - 1) * ps.p + 1:ps.p]
            half, part = divmod(i * 2 + a, ps.across)
            first = part * ps.nw * ps.p + t
            return states[:, half * ps.nb * N:(half + 1) * ps.nb * N].rearrange("p (b n) -> p b n", n=N)[
                :, :, first:first + (ps.nw - 1) * ps.p + 1:ps.p]

        def rounds_of(eng, ps, body):
            if ps.across > 1:
                for i in range(ps.rounds):
                    body(i)
                return
            body(0)
            if ps.rounds > 1:
                with eng.Fori(1, ps.rounds) as i:
                    body(i)

        EB = 2 * GB
        ET = EB * N
        ETURNS = B // EB
        SLOTS = 4

        def slots(name, shape):
            return [sb(f"{name}{i}", shape, side="right", scope=ctx) for i in range(SLOTS)]

        ident_r = sb("ident_r", [128, 128], F32R, side="right", scope=ctx)
        fin, ln3_st, ln3_mv, ln3_ve, ln3_rs, ln3_sh = (slots(n, s) for n, s in (
            ("fin", [N, ET]), ("ln3_st", [N, EB, 6]), ("ln3_mv", [N, EB, 2]), ("ln3_ve", [N, EB]),
            ("ln3_rs", [N, EB]), ("ln3_sh", [N, EB])))
        ident_r_set, sum_mm, st3, mv3, ve3, rs3, rm3, sh3, fin_done = map(sem, (
            "ident_r_set", "sum_mm", "st3", "mv3", "ve3", "rs3", "rm3", "sh3", "fin_done"))
        fin_free = [sem(f"fin_free{i}") for i in range(SLOTS)]
        last_pass = passes[-1]
        gates_total = last_pass.gates_before + last_pass.rounds * last_pass.gates

        assert last_pass.rounds == 2 and last_pass.across == 1

        with nc.Block() as block:
            @block.tensor
            def _(pe):
                for ps in passes:
                    w = [[part[:, ps.p - 1, gate * D:(gate + 1) * D] for gate in range(GATES)]
                         for part in (wih_hi, wih_lo, whh_hi, whh_lo)]
                    out = [[flat(bank[4 * a + gate], ps) for gate in range(GATES)] for a in range(2)]

                    def body(i):
                        if ps.p > 1:
                            prev = passes[ps.p - 2]
                            done = prev_steps(prev, ps, i)
                            for a in range(2):
                                need(pe, h_lo[a], done)
                        for t in range(ps.p):
                            for a in range(2):
                                st = Step(ps, i, t)
                                hi, lo = (nodes_of(s, ps, i, a, t) for s in (st_hi, st_lo))
                                for gate in st.gates:
                                    need(pe, gate_out[a], st.read_before[gate])
                                    pe.matmul(out[a][gate], w[0][gate], hi, start=True, stop=False)
                                    pe.matmul(out[a][gate], w[1][gate], hi, start=False, stop=False)
                                for gate in st.gates:
                                    mm = pe.matmul(out[a][gate], w[0][gate], lo, start=False, stop=st.first)
                                    if st.first:
                                        mm.then_inc(gate_mm[a], 1)
                            if t == 0:
                                continue
                            for a in range(2):
                                st = Step(ps, i, t)
                                hi, lo = flat(mid_hi[a], ps), flat(mid_lo[a], ps)
                                need(pe, h_hi[a], st.n)
                                for gate in st.gates:
                                    pe.matmul(out[a][gate], w[2][gate], hi, start=False, stop=False)
                                    pe.matmul(out[a][gate], w[3][gate], hi, start=False, stop=False)
                                need(pe, h_lo[a], st.n)
                                for gate in st.gates:
                                    pe.matmul(out[a][gate], w[2][gate], lo, start=False, stop=True) \
                                      .then_inc(gate_mm[a], 1)

                    rounds_of(pe, ps, body)

                for g in range(ETURNS):
                    for a in range(2):
                        if g % (ETURNS // 2) == 0:
                            pe.wait_ge(h_lo[a], last_pass.steps_before + last_pass.p * (g // (ETURNS // 2) + 1))
                        if g == a * SLOTS // 2:
                            pe.wait_ge(gate_out[a], gates_total)
                    need(pe, fin_done, g - SLOTS + 1)
                    for half in range(2):
                        out = bank[2 * (g % SLOTS) + half]
                        first = g * EB + half * GB
                        pe.matmul(out[:], ident[:], xres[:, first:first + GB, :].rearrange("p b d -> p (b d)"),
                                  start=True, stop=False)
                        if g == 0 and half == 0:
                            pe.wait_ge(ident_r_set, 1)
                        for b in range(GB):
                            at = slice((first + b) * N, (first + b + 1) * N)
                            for part in (st_hi, st_lo):
                                mm = pe.matmul(out[:, b * D:(b + 1) * D], part[:, at], ident_r[:],
                                               start=False, stop=part is st_lo and b == GB - 1)
                        mm.then_inc(sum_mm, 1)

            @block.scalar
            def _(act):
                tile_of = {I_: act_i, F_: act_f, G_: act_g, O_: act_o}

                def gates_of(ps, st, a):
                    for k, gate in enumerate(st.gates):
                        need(act, gate_mm[a], st.gates_before + k + 1)
                        if gate == O_:
                            need(act, h_full[a], st.n)
                        at = (ps.p - 1) * GATES + gate
                        act.activation(tile_of[gate][a][:, 0:ps.cols], bank[4 * a + gate][:, 0:ps.cols],
                                       ACT.Tanh if gate == G_ else ACT.Sigmoid,
                                       bias=gate_bias[:, at:at + 1]).then_inc(gate_out[a], 1)

                def tanh_of(ps, st, a):
                    need(act, cell_done[a], st.n + 1)
                    need(act, h_lo[a], st.n)
                    act.activation(h_new[a][:, 0:ps.cols], cell[a][:, 0:ps.cols], ACT.Tanh) \
                       .then_inc(tanh_done[a], 1)

                for ps in passes:
                    def body(i):
                        for t in range(ps.p):
                            st = Step(ps, i, t)
                            for a in range(2):
                                gates_of(ps, st, a)
                            for a in range(2):
                                tanh_of(ps, st, a)

                    rounds_of(act, ps, body)

                for u in range(SLOTS):
                    act.sem_inc(fin_free[u], 16)
                with act.Fori(0, ETURNS // SLOTS) as m:
                    for u in range(SLOTS):
                        act.wait_ge(sh3, m * SLOTS + (u + 1))
                        act.wait_ge(fin_free[u], m * 16 + 16)
                        for b in range(EB):
                            at = slice(b % GB * D, (b % GB + 1) * D)
                            op = act.activation(fin[u][:, b * D:(b + 1) * D], bank[2 * u + b // GB][:, at],
                                                ACT.Identity, bias=ln3_sh[u][:, b:b + 1], scale=ln3_rs[u][:, b:b + 1])
                        op.then_inc(fin_done, 1)

            @block.vector
            def _(dve):
                dve.tensor_copy(ident_r[:], ident[:]).then_inc(ident_r_set, 1)

                def cell_of(ps, st, a):
                    c = slice(0, ps.cols)
                    if st.first:
                        need(dve, gate_out[a], st.gates_before + 2)
                        dve.tensor_tensor(cell[a][:, c], act_i[a][:, c], act_g[a][:, c], ALU.mult) \
                           .then_inc(cell_done[a], 1)
                        return
                    need(dve, gate_out[a], st.gates_before + 1)
                    dve.tensor_tensor(fc[a][:, c], act_f[a][:, c], cell[a][:, c], ALU.mult) \
                       .then_inc(cell_ops[a], 1)
                    need(dve, gate_out[a], st.gates_before + 3)
                    dve.tensor_tensor(act_i[a][:, c], act_i[a][:, c], act_g[a][:, c], ALU.mult) \
                       .then_inc(cell_ops[a], 1)
                    need(dve, cell_ops[a], st.mids * 2 + 2)
                    dve.tensor_tensor(cell[a][:, c], act_i[a][:, c], fc[a][:, c], ALU.add) \
                       .then_inc(cell_done[a], 1)

                def state_of(ps, st, a, i):
                    c = slice(0, ps.cols)
                    need(dve, tanh_done[a], st.n + 1)
                    dve.tensor_tensor(nodes_of(st_hi, ps, i, a, st.t) if st.last else flat(mid_hi[a], ps),
                                      flat(act_o[a], ps), flat(h_new[a], ps), ALU.mult).then_inc(h_hi[a], 1)
                    dve.tensor_tensor(h_new[a][:, c], act_o[a][:, c], h_new[a][:, c], ALU.mult) \
                       .then_inc(h_full[a], 1)

                for ps in passes:
                    def body(i):
                        for t in range(ps.p):
                            st = Step(ps, i, t)
                            for a in range(2):
                                cell_of(ps, st, a)
                            for a in range(2):
                                state_of(ps, st, a, i)

                    rounds_of(dve, ps, body)

                with dve.Fori(0, ETURNS // SLOTS) as m:
                    for u in range(SLOTS):
                        g = m * SLOTS + u
                        for b in range(EB):
                            if b % GB == 0:
                                dve.wait_ge(sum_mm, g * 2 + (b // GB + 1))
                            at = slice(b % GB * D, (b % GB + 1) * D)
                            dve.bn_stats(ln3_st[u][:, b, :], bank[2 * u + b // GB][:, at]).then_inc(st3, 1)
                        dve.wait_ge(st3, (g + 1) * EB)
                        dve.memset(idle_words[:, u:u + 1], 0.0)
                        for b in range(EB):
                            dve.bn_aggr(ln3_mv[u][:, b, :], ln3_st[u][:, b, :]).then_inc(mv3, 1)

            @block.gpsimd
            def _(pool):
                for ps in passes:
                    def body(i):
                        for t in range(ps.p):
                            for a in range(2):
                                st = Step(ps, i, t)
                                hi, lo = ((nodes_of(s, ps, i, a, t) for s in (st_hi, st_lo)) if st.last else
                                          (flat(mid_hi[a], ps), flat(mid_lo[a], ps)))
                                need(pool, h_full[a], st.n + 1)
                                pool.tensor_tensor(lo, flat(h_new[a], ps), hi.bitcast(F32), ALU.subtract) \
                                    .then_inc(h_lo[a], 1)

                    rounds_of(pool, ps, body)

                with pool.Fori(0, ETURNS // SLOTS) as m:
                    for u in range(SLOTS):
                        g = m * SLOTS + u
                        mean, var = ln3_mv[u][:, :, 0], ln3_mv[u][:, :, 1]
                        pool.wait_ge(mv3, (g + 1) * EB)
                        pool.tensor_tensor(ln3_ve[u][:], var, eps_wide[:], ALU.add).then_inc(ve3, 1)
                        pool.wait_ge(ve3, g + 1)
                        pool.tensor_tensor(ln3_rs[u][:], ln3_ve[u][:], neg_half_wide[:], ALU.pow).then_inc(rs3, 1)
                        pool.wait_ge(rs3, g + 1)
                        pool.tensor_tensor(ln3_sh[u][:], mean, ln3_rs[u][:], ALU.mult).then_inc(rm3, 1)
                        pool.wait_ge(rm3, g + 1)
                        pool.tensor_tensor(ln3_sh[u][:], zero_wide[:], ln3_sh[u][:], ALU.subtract).then_inc(sh3, 1)

            @block.sync
            def _(sp):
                with sp.Fori(0, ETURNS // SLOTS) as m:
                    for u in range(SLOTS):
                        sp.wait_ge(fin_done, m * SLOTS + (u + 1))
                        sp.dma_start(io["out"][:, ds((m * SLOTS + u) * ET, ET)], fin[u][:]).then_inc(fin_free[u], 16)
                for u in range(SLOTS):
                    sp.wait_ge(fin_free[u], 16 * (1 + ETURNS // SLOTS))


_DRAM = (("x", (N, B * D)), ("xt", (D, TOKENS)), ("adj", (N, N)), ("adjt", (N, N)), ("wqkv", (D, 3 * D)),
         ("w_l1", (D, 3, D)), ("rows", (1, 3, D)), ("w1t", (D, HID * 128)), ("w2t", (128, HID, D)),
         ("wg", (D, 2, D)), ("lstm_w", (D, 2 * STEPS * GATES * D)),
         ("bn1p", (128, 3, HID)), ("bn2p", (128, 3)), ("lstm_b", (D, 2, STEPS * GATES)))


def kernel(**inputs):
    import numpy as np
    import concourse.bacc as bacc
    from concourse.bass_utils import run_bass_kernel_spmd

    a = {k: np.asarray(v) for k, v in inputs.items()}
    cols = lambda v: v.reshape(-1, 128).T
    gates_t = lambda w: w.transpose(2, 0, 1).reshape(D, -1)
    laid = {
        "x": a["x"].transpose(1, 0, 2).reshape(N, B * D),
        "xt": a["x"].transpose(2, 0, 1).reshape(D, TOKENS),
        "adj": a["adj"], "adjt": a["adj"].T, "wqkv": a["L0_gnn_W"],
        "w_l1": a["L1_gnn_W"].transpose(1, 0, 2),
        "rows": np.stack([a["L1_gnn_bias"], a["L3_gnn_bg0"], a["L3_gnn_bg1"]])[None],
        "w1t": a["L2_gnn_W1"].T,
        "w2t": a["L2_gnn_W2"].T.reshape(HID, 128, D).transpose(1, 0, 2),
        "wg": np.stack([a["L3_gnn_Wg0"], a["L3_gnn_Wg1"]], axis=1),
        "lstm_w": np.concatenate([gates_t(a["L3_gnn_Wih"]), gates_t(a["L3_gnn_Whh"])], axis=1),
        "bn1p": np.stack([cols(a[f"L2_gnn_{n}"]) for n in ("b1", "g1", "be1")], axis=1),
        "bn2p": np.concatenate([cols(a[f"L2_gnn_{n}"]) for n in ("b2", "g2", "be2")], axis=1),
        "lstm_b": np.stack([cols(a["L3_gnn_bih"].reshape(-1)), cols(a["L3_gnn_bhh"].reshape(-1))], axis=1),
    }
    laid = {k: np.ascontiguousarray(v) for k, v in laid.items()}

    nc = bacc.Bacc("TRN2", target_bir_lowering=False, num_devices=1)
    io = {n: nc.dram_tensor(f"in_{n}", s, F32, kind="ExternalInput").ap() for n, s in _DRAM}
    io["out"] = nc.dram_tensor("out", (N, B * D), F32, kind="ExternalOutput").ap()
    build(nc, io)
    r = run_bass_kernel_spmd(nc, [{f"in_{n}": v for n, v in laid.items()}], core_ids=[0])
    return np.ascontiguousarray(r.results[0]["out"].reshape(N, B, D).transpose(1, 0, 2))
```
